# Optimizing a Trainium2 kernel written in Bass

```python
import numpy as np
import jax
import jax.numpy as jnp

def _softmax(x, axis=-1):
    return jax.nn.softmax(x, axis=axis)

def _gelu(x):
    return jax.nn.gelu(x, approximate=True)

def _silu(x):
    return jax.nn.silu(x)

def _sigmoid(x):
    return jax.nn.sigmoid(x)

def _layernorm(x, axis=-1, eps=1e-05):
    m = jnp.mean(x, axis=axis, keepdims=True)
    v = jnp.var(x, axis=axis, keepdims=True)
    return (x - m) / jnp.sqrt(v + eps)

def _scatter_add(tgt, idx, src, axis=0):
    return tgt.at[idx].add(src)

def _segment_sum(src, seg, n):
    return jax.ops.segment_sum(src, seg, n)
kernel_name = 'mk_gnn_ffn_d1_gnn_r8_e6029a'

def setup_inputs(seed: int=0):
    np.random.seed(seed)
    _w = jnp.asarray

    def _rec_inputs():
        import jax
        import jax.numpy as jnp
        _gk = jax.random.key(seed)
        x = -0.0003713 + 1 * jax.random.normal(jax.random.fold_in(_gk, 1), (12500, 256), jnp.float32)
        src = jax.random.randint(jax.random.fold_in(_gk, 2), (200000,), 0, 12500, jnp.int32)
        dst = jnp.minimum((12500 * jax.random.uniform(jax.random.fold_in(_gk, 3), (200000,)) ** 2.0).astype(jnp.int32), 99999)
        _o = jnp.argsort(dst, stable=True)
        src = src[_o]
        dst = dst[_o]
        edge_weight = jax.random.uniform(jax.random.fold_in(_gk, 12), (200000,), jnp.float32, 0.0, 0.999999)
        return (x, src, dst, edge_weight)
    x, src, dst, edge_weight = _rec_inputs()

    def _L0_gnn_setup():
        import jax, jax.numpy as jnp
        import numpy as np
        N_NODES = 6250
        N_EDGES = 200000
        F_IN = 256
        F_OUT = 256

        def _gcn_conv(x, src, dst, ew, W, b, n_nodes):
            xW = x @ W
            deg = jax.ops.segment_sum(ew, dst, num_segments=n_nodes) + 1.0
            dinv = jnp.where(deg > 0, jax.lax.rsqrt(deg), 0.0)
            norm = dinv[src] * ew * dinv[dst]
            agg = jax.ops.segment_sum(norm[:, None] * xW[src], dst, num_segments=n_nodes)
            agg = agg + (dinv * dinv)[:, None] * xW
            return agg + b
        key = jax.random.key(seed)
        ks = jax.random.split(key, 7)
        x = jax.random.normal(ks[0], (N_NODES, F_IN), dtype=jnp.float32)
        edge_index = jax.random.randint(ks[1], (2, N_EDGES), 0, N_NODES, dtype=jnp.int64)
        edge_weight = jax.random.uniform(ks[2], (N_EDGES,), dtype=jnp.float32)
        W1 = jax.random.normal(ks[3], (F_IN, F_OUT), dtype=jnp.float32) * (1.0 / np.sqrt(F_IN))
        b1 = jnp.zeros((F_OUT,), dtype=jnp.float32)
        W2 = jax.random.normal(ks[4], (F_OUT, F_OUT), dtype=jnp.float32) * (1.0 / np.sqrt(F_OUT))
        b2 = jnp.zeros((F_OUT,), dtype=jnp.float32)
        return {'x': x, 'edge_index': edge_index, 'edge_weight': edge_weight, 'W1': W1, 'b1': b1, 'W2': W2, 'b2': b2}
    _L0_gnn_all = _L0_gnn_setup()
    _L0_gnn_in = {k: v for k, v in _L0_gnn_all.items() if k in ('W1', 'b1', 'W2', 'b2')}
    del _L0_gnn_all

    def _L0_ffn_setup():
        import jax, jax.numpy as jnp
        import numpy as np
        NUM_EXPERTS = 8
        TOP_K = 2
        B, S, D = (8, 1024, 256)

        def _moe(tokens, router_w, w1, b1, w2, b2):
            N = tokens.shape[0]
            E = router_w.shape[0]
            logits = tokens.astype(jnp.float32) @ router_w.astype(jnp.float32).T
            probs = jax.nn.softmax(logits, axis=-1)
            rw, re = jax.lax.top_k(probs, TOP_K)
            if TOP_K > 1:
                rw = rw / jnp.maximum(rw.sum(-1, keepdims=True), 1e-12)
            rw = rw.astype(tokens.dtype)
            combine = jnp.zeros((N, E), tokens.dtype).at[jnp.arange(N)[:, None], re].set(rw)
            out = tokens
            for e in range(E):
                h = jax.nn.gelu(tokens @ w1[e] + b1[e], approximate=False)
                y = h @ w2[e] + b2[e]
                out = out + combine[:, e:e + 1] * y
            return out
        key = jax.random.key(seed)
        ks = jax.random.split(key, 4)
        scale = 1.0 / np.sqrt(D).astype(np.float32)
        return {'input_embeddings': jax.random.normal(ks[0], (B, S, D), jnp.float32), 'router_w': jax.random.normal(ks[1], (NUM_EXPERTS, D), jnp.float32) * scale, 'w1': jax.random.normal(ks[2], (NUM_EXPERTS, D, D), jnp.float32) * scale, 'b1': jnp.zeros((NUM_EXPERTS, D), jnp.float32), 'w2': jax.random.normal(ks[3], (NUM_EXPERTS, D, D), jnp.float32) * scale, 'b2': jnp.zeros((NUM_EXPERTS, D), jnp.float32)}
    _L0_ffn_all = _L0_ffn_setup()
    _L0_ffn_in = {k: v for k, v in _L0_ffn_all.items() if k in ('router_w', 'w1', 'b1', 'w2', 'b2')}
    del _L0_ffn_all
    return {'x': x, 'src': src, 'dst': dst, 'edge_weight': edge_weight, 'L0_gnn_W1': _L0_gnn_in['W1'], 'L0_gnn_b1': _L0_gnn_in['b1'], 'L0_gnn_W2': _L0_gnn_in['W2'], 'L0_gnn_b2': _L0_gnn_in['b2'], 'L0_ffn_router_w': _L0_ffn_in['router_w'], 'L0_ffn_w1': _L0_ffn_in['w1'], 'L0_ffn_b1': _L0_ffn_in['b1'], 'L0_ffn_w2': _L0_ffn_in['w2'], 'L0_ffn_b2': _L0_ffn_in['b2']}

def reference(x, src, dst, edge_weight, L0_gnn_W1, L0_gnn_b1, L0_gnn_W2, L0_gnn_b2, L0_ffn_router_w, L0_ffn_w1, L0_ffn_b1, L0_ffn_w2, L0_ffn_b2):
    import jax
    import jax.numpy as jnp

    def _L0_gnn_ref(x, edge_index, edge_weight, W1, b1, W2, b2):
        import jax, jax.numpy as jnp
        import numpy as np
        N_NODES = 6250
        N_EDGES = 200000
        F_IN = 256
        F_OUT = 256

        def _gcn_conv(x, src, dst, ew, W, b, n_nodes):
            xW = x @ W
            deg = jax.ops.segment_sum(ew, dst, num_segments=n_nodes) + 1.0
            dinv = jnp.where(deg > 0, jax.lax.rsqrt(deg), 0.0)
            norm = dinv[src] * ew * dinv[dst]
            agg = jax.ops.segment_sum(norm[:, None] * xW[src], dst, num_segments=n_nodes)
            agg = agg + (dinv * dinv)[:, None] * xW
            return agg + b
        src = edge_index[0]
        dst = edge_index[1]
        n = x.shape[0]
        h1 = jax.nn.relu(_gcn_conv(x, src, dst, edge_weight, W1, b1, n))
        h2 = jax.nn.relu(_gcn_conv(h1, src, dst, edge_weight, W2, b2, n))
        return h2

    def _L0_ffn_ref(input_embeddings, router_w, w1, b1, w2, b2):
        import jax, jax.numpy as jnp
        import numpy as np
        NUM_EXPERTS = 8
        TOP_K = 2
        B, S, D = (8, 1024, 256)

        def _moe(tokens, router_w, w1, b1, w2, b2):
            N = tokens.shape[0]
            E = router_w.shape[0]
            logits = tokens.astype(jnp.float32) @ router_w.astype(jnp.float32).T
            probs = jax.nn.softmax(logits, axis=-1)
            rw, re = jax.lax.top_k(probs, TOP_K)
            if TOP_K > 1:
                rw = rw / jnp.maximum(rw.sum(-1, keepdims=True), 1e-12)
            rw = rw.astype(tokens.dtype)
            combine = jnp.zeros((N, E), tokens.dtype).at[jnp.arange(N)[:, None], re].set(rw)
            out = tokens
            for e in range(E):
                h = jax.nn.gelu(tokens @ w1[e] + b1[e], approximate=False)
                y = h @ w2[e] + b2[e]
                out = out + combine[:, e:e + 1] * y
            return out
        b, s, d = input_embeddings.shape
        tokens = input_embeddings.reshape(b * s, d)
        return _moe(tokens, router_w, w1, b1, w2, b2).reshape(b, s, d)
    edge_index = jnp.stack([src, dst])
    x = x + _L0_gnn_ref(_layernorm(x, axis=-1), edge_index, edge_weight, L0_gnn_W1, L0_gnn_b1, L0_gnn_W2, L0_gnn_b2)
    x = x + _L0_ffn_ref(_layernorm(x, axis=-1)[None], L0_ffn_router_w, L0_ffn_w1, L0_ffn_b1, L0_ffn_w2, L0_ffn_b2)[0]
    return x

_drawn_inputs = setup_inputs


def setup_inputs(seed=0):
    import zlib

    import numpy as np

    out = dict(_drawn_inputs(seed))
    spreads = {'L0_gnn_b1': (0.0, 0.1),
     'L0_gnn_b2': (0.0, 0.1),
     'L0_ffn_b1': (0.0, 0.327),
     'L0_ffn_b2': (0.0, 0.1)}
    factors = {}
    for name, (base, spread) in spreads.items():
        noise = np.random.default_rng([zlib.crc32(name.encode()), seed]).standard_normal(out[name].shape)
        drawn = base * np.exp(spread * noise) if base else spread * noise
        out[name] = jnp.asarray(drawn.astype(out[name].dtype))
    for name, factor in factors.items():
        out[name] = (out[name] * factor).astype(out[name].dtype)
    return out
```

```python
from contextlib import ExitStack

import concourse.bass as bass
from concourse import mybir

F32 = mybir.dt.float32
I32 = mybir.dt.int32
U32 = mybir.dt.uint32
ALU = mybir.AluOpType
ACT = mybir.ActivationFunctionType
AX = mybir.AxisListType

P = 128
N, D, NEDGE, NEXP = 12500, 256, 200000, 8
KD = D // P
NB = -(-N // P)
NP = NB * P
LAST = N - (NB - 1) * P
GE = 256
GT = GE // P
R = 8
NI = 98
NG = NI * R
NT = NG * GT
W = 64
GQ = 112
GC = NG // GQ
FULLC = NEDGE // (GQ * GE)
REST = NEDGE - FULLC * GQ * GE
RESTQ, RESTE = REST // GE, REST % GE
ACCW = NP + W
REC = 20
REC_E, REC_X, REC_B = 0, 2, 12
EPS = 1e-5
CH = 40
XS = 7
BIG = 1.0e6

assert NG * GE >= NEDGE and FULLC == GC - 1 and R * GT == 16


def build(nc, x, src, dst, ew, gw1, gb1, gw2, gb2, rw, ew1, eb1, ew2, eb2, out):
    ctx = ExitStack()

    def sb(name, shape, dt=F32):
        return ctx.enter_context(nc.sbuf_tensor(name, shape, dt))

    def pb(name):
        return ctx.enter_context(nc.psum_tensor(name, [P, 512], F32))

    def sem(name):
        return ctx.enter_context(nc.semaphore(name))

    ytab = [nc.dram_tensor(f"ytab{l}", [NP, D], F32).ap() for l in range(2)]
    gtab = nc.dram_tensor("gtab", [3, NG], F32).ap()

    accbuf = sb("accbuf", [P, KD * ACCW])
    accT = accbuf[:, :].rearrange("p (k n) -> p k n", k=KD)
    at = [0]

    def early(words):
        v = accbuf[:, at[0]:at[0] + words]
        at[0] += words
        return v

    GW = GC * GE
    dst_i = early(GW)[0:GQ, :].bitcast(I32).rearrange("q (c e) -> q c e", c=GC)
    src_i = early(GW)[0:GQ, :].bitcast(I32).rearrange("q (c e) -> q c e", c=GC)
    ew_g = early(GW)[0:GQ, :].rearrange("q (c e) -> q c e", c=GC)
    dst_f = early(GW)[0:GQ, :].rearrange("q (c e) -> q c e", c=GC)
    src_f = early(GW)[0:GQ, :].rearrange("q (c e) -> q c e", c=GC)
    rel_g = early(GW)[0:GQ, :].rearrange("q (c e) -> q c e", c=GC)
    dstT = early(NT)
    digit_i = early(NT).bitcast(I32)
    dst_i32 = early(NT).bitcast(I32)
    loT = early(NT)
    hiT = early(NT)
    rows = early(3 * NG)[0:1, :].rearrange("o (t g) -> o t g", t=3)
    ones_row = early(NG)[0:1, :]
    xcum = early(NG + 1)[0:1, :]
    least = early(2 * (NI + P))[0:1, :].rearrange("o (a n) -> o a n", a=2)
    assert at[0] <= KD * ACCW

    srcT = sb("srcT", [P, NT], I32)
    relT = sb("relT", [P, NT])
    ewT = sb("ewT", [P, NT])
    msg = sb("msg", [P, R * GT, D])
    idx = sb("idx", [P, R * GT], I32)
    sel = sb("sel", [P, R * GT, W])
    xin, y1 = msg[:, 0:XS, :], msg[:, XS:2 * XS, :]
    selw = sel[:, :, :].rearrange("p c w -> p (c w)")
    onelo = selw[:, 0:4 * P].rearrange("p (k n) -> p k n", k=4)
    onehi = selw[:, 4 * P:4 * (P + NB)].rearrange("p (k n) -> p k n", k=4)
    xsel = sb("xsel", [P, GT, W])
    xrel = sb("xrel", [P, GT])
    ident = sb("ident", [P, P])
    iota = sb("iota", [P, P])
    gmin = sb("gmin", [GQ, GC])
    gmax = sb("gmax", [GQ, GC])
    ints = sb("ints", [GQ, GC], I32)
    gbase = sb("gbase", [GQ, GC])
    gextra = sb("gextra", [GQ, GC])
    eint = sb("eint", [1, NI + 1], I32)
    rec = sb("rec", [1, NI, REC], I32)
    dinv = sb("dinv", [P, NB])
    mv = sb("mv", [P, NB, 2])
    mv7 = sb("mv7", [P, XS, 2])
    hiew = sb("hiew", [P, 2, 8])
    stats = sb("stats", [P, XS, 6])
    lnscale = sb("lnscale", [P, NB])
    lnbias = sb("lnbias", [P, NB])
    gw = [sb(f"gw{l}", [P, KD, D]) for l in range(2)]
    gb = [sb(f"gb{l}", [P, D]) for l in range(2)]
    rwT = sb("rwT", [P, KD, NEXP])
    rw_s = sb("rw_s", [NEXP, D])
    w1_s = sb("w1_s", [P, NEXP, KD, D])
    w2_s = sb("w2_s", [P, NEXP, KD, D])
    b1_s = sb("b1_s", [P, NEXP, KD])
    b1_r = sb("b1_r", [NEXP * KD, P])
    b2_s = sb("b2_s", [NEXP, D])
    aggS = sb("aggS", [P, KD, P])
    lin = sb("lin", [P, D])
    yS = sb("yS", [P, D])
    xS = sb("xS", [P, D])
    x2 = sb("x2", [P, D])
    tok = sb("tok", [P, D])
    tokT = sb("tokT", [P, KD, P])
    res = sb("res", [P, D])
    st1 = sb("st1", [P, 6])
    mv1 = sb("mv1", [P, 2])
    var1 = sb("var1", [P, 1])
    halfi = sb("halfi", [P, 1], I32)
    rs = sb("rs", [P, 1])
    nt1 = sb("nt1", [P, 1])
    nt2 = sb("nt2", [P, 1])
    lg = sb("lg", [P, NEXP])
    top = sb("top", [P, 8])
    topi = sb("topi", [P, 8], U32)
    topf = sb("topf", [P, 2])
    gap = sb("gap", [P, 1])
    th = sb("th", [P, 1])
    wts = sb("wts", [P, 2])
    pick = sb("pick", [P, NEXP])
    comb = sb("comb", [P, NEXP])
    combT = sb("combT", [NEXP, P])
    hS = sb("hS", [P, 2, KD, P])

    part = [pb(f"part{i}") for i in range(2)]
    psG, psT = pb("psG"), pb("psT")
    psH = [pb(f"psH{i}") for i in range(2)]
    psY = [pb(f"psY{i}") for i in range(2)]
    y1banks = [*part, psG, *psH, *psY]

    E = mybir.EngineType
    held = {e: sem(f"held_{n}") for e, n in ((nc.vector, "dve"), (nc.scalar, "act"), (nc.tensor, "pe"), (nc.sync, "sp"), (nc.gpsimd, "pool"))}

    def hold(eng):
        eng.sem_inc(held[eng], 1)

    s_pads = sem("s_pads")
    s_edges = sem("s_edges")
    s_const = sem("s_const")
    s_wts = sem("s_wts")
    s_chain = sem("s_chain")
    s_gout = sem("s_gout")
    s_grow = sem("s_grow")
    s_gready = sem("s_gready")
    s_edgeT = sem("s_edgeT")
    s_edgeC = sem("s_edgeC")
    s_rec = sem("s_rec")
    s_digits = sem("s_digits")
    s_onelo = sem("s_onelo")
    s_onehi = sem("s_onehi")
    s_hiew = sem("s_hiew")
    s_degmm = sem("s_degmm")
    s_deg = sem("s_deg")
    s_rwt = sem("s_rwt")
    s_xin = [sem(f"s_xin{i}") for i in range(XS)]
    s_xused = sem("s_xused")
    s_mv = sem("s_mv")
    s_std = sem("s_std")
    s_var = sem("s_var")
    s_y1 = sem("s_y1")
    s_y1T = sem("s_y1T")
    s_y1C = sem("s_y1C")
    s_y1out = [sem(f"s_y1out{i}") for i in range(XS)]
    s_msg = [sem(f"s_msg{r}") for r in range(R)]
    s_idx = [sem(f"s_idx{h}") for h in range(2)]
    s_free = sem("s_free")
    s_sel = sem("s_sel")
    s_part = sem("s_part")
    s_added = sem("s_added")
    s_iter = sem("s_iter")
    s_xsel = [sem(f"s_xsel{l}") for l in range(2)]
    s_xpart = [sem(f"s_xpart{l}") for l in range(2)]
    s_xadd = [sem(f"s_xadd{l}") for l in range(2)]
    s_agg = [sem(f"s_agg{l}") for l in range(2)]
    s_lin = [sem(f"s_lin{l}") for l in range(2)]
    s_bch = [sem(f"s_bch{l}") for l in range(2)]
    s_y2 = sem("s_y2")
    s_y2T = sem("s_y2T")
    s_y2C = sem("s_y2C")
    s_y2out = sem("s_y2out")
    s_x = sem("s_x")
    s_tok = sem("s_tok")
    s_tokT = sem("s_tokT")
    s_tokC = sem("s_tokC")
    s_lg = sem("s_lg")
    s_gap = sem("s_gap")
    s_th = sem("s_th")
    s_comb = sem("s_comb")
    s_combT = sem("s_combT")
    s_combC = sem("s_combC")
    s_b2 = sem("s_b2")
    s_b2add = sem("s_b2add")
    s_h = sem("s_h")
    s_gelu = sem("s_gelu")
    s_y = sem("s_y")
    s_yadd = sem("s_yadd")
    s_out = sem("s_out")

    block = ctx.enter_context(nc.Block())

    def record(eng, i, at, n, top_value):
        _, v = nc.values_load_multi_w_load_instructions(
            rec[0:1, bass.ds(i, 1), at:at + n].rearrange("o i n -> o (i n)"), engines=[eng.engine], min_val=0, max_val=top_value)
        return v

    NTR = 4 * GC

    @block.sync
    def _(sp):
        sp.wait_ge(s_pads, 1)
        for dram, tile in ((dst, dst_i), (src, src_i), (ew, ew_g)):
            sp.dma_start(tile[:, 0:FULLC, :], dram[0:FULLC * GQ * GE].rearrange("(c q e) -> q c e", q=GQ, e=GE)).then_inc(s_edges, 16)
            tail = dram[FULLC * GQ * GE:FULLC * GQ * GE + RESTQ * GE]
            sp.dma_start(tile[0:RESTQ, FULLC, :], tail.rearrange("(q e) -> q e", e=GE)).then_inc(s_edges, 16)
            sp.dma_start(tile[RESTQ:RESTQ + 1, FULLC, 0:RESTE], dram[NEDGE - RESTE:NEDGE].rearrange("(a e) -> a e", a=1)).then_inc(s_edges, 16)
        sp.wait_ge(s_gout, 3)
        with nc.allow_non_contiguous_dma(reason="784 words, once"):
            for n, t in enumerate((gmin, gbase, gextra)):
                sp.dma_start(gtab[n, :].rearrange("(c q) -> q c", q=GQ), t[:, :]).then_inc(s_grow, 16)
        sp.wait_ge(s_grow, 48)
        sp.dma_start(rows[:, :, :], gtab.rearrange("(o t) g -> o t g", o=1)).then_inc(s_gready, 16)
        def load_x(turn, j, k, n):
            sp.wait_ge(s_xused, (j + turn * (NB // XS)) * XS + k + 1)
            hold(sp)
            sp.dma_start(xin[0:n, k, :], x[bass.ds(j * (XS * P) + k * P, n), :]).then_inc(s_xin[k], 16)

        def store_y1(j, k):
            sp.wait_ge(s_y1, j * XS + k + 1)
            hold(sp)
            sp.dma_start(ytab[0][bass.ds(j * (XS * P) + k * P, P), :], y1[:, k, :]).then_inc(s_y1out[k], 16)

        with sp.Fori(0, NB // XS - 1) as j:
            for k in range(XS):
                load_x(0, j, k, P)
        for k in range(XS):
            load_x(0, NB // XS - 1, k, P if k < XS - 1 else LAST)
        for k in range(XS):
            load_x(1, 0, k, P)
        def turn(j, rows_of_last):
            for k in range(XS):
                store_y1(j - 1, k)
            for k in range(XS):
                sp.wait_ge(s_y1out[k], j * 16)
                hold(sp)
                load_x(1, j, k, P if k < XS - 1 else rows_of_last)

        with sp.Fori(1, NB // XS - 1) as j:
            turn(j, P)
        turn(NB // XS - 1, LAST)
        for k in range(XS):
            store_y1(NB // XS - 1, k)
        HC = R * GT // 2

        def stage(l, i, first):
            for h in range(2):
                if not first:
                    for r in range(R // 2):
                        sp.wait_ge(s_msg[h * R // 2 + r], (i + l * NI) * (16 * GT))
                        hold(sp)
                sp.dma_start(idx[:, h * HC:(h + 1) * HC], srcT[:, bass.ds(i * (2 * HC) + h * HC, HC)]).then_inc(s_idx[h], 16)

        sp.wait_ge(s_edgeC, NTR)
        stage(0, 0, True)
        with sp.Fori(1, NI) as i:
            stage(0, i, False)
        with sp.Fori(0, NI) as i:
            stage(1, i, False)

    @block.gpsimd
    def _(pool):
        pool.memset(ident[:, :], 0.0).then_inc(s_const, 1)
        pool.iota(iota[:, :], [[1, P]], base=0, channel_multiplier=0, allow_small_or_imprecise_dtypes=True).then_inc(s_const, 1)
        pool.wait_ge(s_const, 2)
        pool.affine_select(out=ident[:, :], in_=ident[:, :], compare_op=ALU.not_equal, fill=1.0, base=0,
                           pattern=[[-1, P]], channel_multiplier=1).then_inc(s_const, 1)
        pool.wait_ge(s_digits, 1)
        with pool.Fori(0, NT // 8) as j:
            pool.tensor_copy(hiew[:, 0, :], hiT[:, bass.ds(j * 8, 8)]).then_inc(s_hiew, 1)
            pool.tensor_copy(hiew[:, 1, :], ewT[:, bass.ds(j * 8, 8)]).then_inc(s_hiew, 1)
            pool.wait_ge(s_hiew, j * 2 + 2)
            hold(pool)
            for k in range(8):
                pool.wait_ge(s_degmm, j * 8 + k + 1)
                hold(pool)
                pool.tensor_scalar(onehi[:, k % 4, :], iota[:, 0:NB], hiew[:, 0, k:k + 1], hiew[:, 1, k:k + 1],
                                   ALU.is_equal, ALU.mult).then_inc(s_onehi, 1)
            pool.wait_ge(s_onehi, j * 8 + 8)
            hold(pool)
        for l in range(2):
            if l == 0:
                for k in range(XS):
                    pool.wait_ge(s_y1out[k], NB // XS * 16)
                pool.wait_ge(s_y1C, NB + XS)
            else:
                pool.wait_ge(s_y2out, (NB + 1) * 16)
            with pool.Fori(0, NI) as i:
                for r in range(R):
                    pool.wait_ge(s_free, (i + l * NI) * R + r + 1)
                    hold(pool)
                    if r % (R // 2) == 0:
                        pool.wait_ge(s_idx[r // (R // 2)], (i + l * NI) * 16 + 16)
                        hold(pool)
                    for j in range(GT):
                        c = r * GT + j
                        pool.indirect_dma_start(msg[:, c, :], None, ytab[l], bass.IndirectOffsetOnAxis(
                            ap=idx[:, c:c + 1].bitcast(U32), axis=0)).then_inc(s_msg[r], 16)

    @block.scalar
    def _(act):
        for l, (w, b) in enumerate(((gw1, gb1), (gw2, gb2))):
            act.dma_start(gw[l][:, :, :], w.rearrange("(k p) n -> p k n", p=P)).then_inc(s_wts, 16)
            act.dma_start(gb[l][:, :], b.rearrange("(o n) -> o n", o=1).broadcast_to([P, D])).then_inc((s_y2out, s_out)[l], 16)
        act.dma_start(rw_s[:, :], rw).then_inc(s_wts, 16)
        act.dma_start(b1_r[:, :], eb1.rearrange("e (k p) -> (e k) p", p=P)).then_inc(s_wts, 16)
        act.dma_start(b2_s[:, :], eb2).then_inc(s_wts, 16)
        act.dma_start(w1_s[:, :, :, :], ew1.rearrange("e (k p) n -> p e k n", p=P)).then_inc(s_wts, 16)
        act.dma_start(w2_s[:, :, :, :], ew2.rearrange("e (k p) n -> p e k n", p=P)).then_inc(s_wts, 16)
        for n in range(NTR):
            a, c = n // GC, n % GC
            tile = (dstT, relT, ewT, srcT)[a]
            act.wait_ge(s_edgeT, n + 1)
            act.activation(tile[:, c * GQ * GT:(c + 1) * GQ * GT].rearrange("p (q j) -> p j q", j=GT),
                           (psH[n % 2])[:, 0:GT * GQ].rearrange("p (j q) -> p j q", j=GT), ACT.Copy).then_inc(s_edgeC, 1)
        act.wait_ge(s_rwt, 1)
        act.activation(rwT[:, :, :].rearrange("p k e -> p (k e)"), psG[:, 0:KD * NEXP], ACT.Copy).then_inc(s_rwt, 1)
        act.activation(b1_s[:, :, :].rearrange("p e k -> p (e k)"), psG[:, 32:32 + NEXP * KD], ACT.Copy).then_inc(s_rwt, 1)
        act.wait_ge(s_var, 2)
        act.activation(dinv[:, :], dinv[:, :], ACT.Sqrt).then_inc(s_std, 1)
        act.activation(lnscale[:, :], lnscale[:, :], ACT.Sqrt).then_inc(s_std, 1)
        with act.Fori(0, NB // XS) as j:
            for k in range(XS):
                act.wait_ge(s_y1T, j * XS + k + 1)
                hold(act)
                act.activation(accT[:, :, bass.ds(j * (XS * P) + k * P, P)],
                               y1banks[k][:, 0:D].rearrange("p (k n) -> p k n", k=KD), ACT.Copy).then_inc(s_y1C, 1)

        def sums(l, b):
            act.wait_ge(s_lin[l], b + 1)
            hold(act)
            act.activation(aggS[:, :, :], accT[:, :, bass.ds(b * P, P)], ACT.Copy).then_inc(s_agg[l], 1)

        def block0(b):
            sums(0, b)
            act.wait_ge(s_y2, b + 2)
            hold(act)
            act.dma_start(ytab[1][bass.ds(b * P, P), :], yS[:, :]).then_inc(s_y2out, 16)
            act.wait_ge(s_y2T, b + 2)
            act.wait_ge(s_agg[0], b + 1)
            hold(act)
            act.activation(accT[:, :, bass.ds(b * P, P)], psT[:, 0:D].rearrange("p (k n) -> p k n", k=KD),
                           ACT.Copy).then_inc(s_y2C, 1)

        def block1(b, n):
            sums(1, b)
            act.wait_ge(s_b2add, b + 1)
            hold(act)
            act.dma_start(xS[0:n, :], x[bass.ds(b * P, n), :]).then_inc(s_x, 16)
            act.wait_ge(s_tokT, b + 1)
            act.wait_ge(s_y, b * NEXP + 2)
            hold(act)
            act.activation(tokT[:, :, :], psT[:, 0:D].rearrange("p (k n) -> p k n", k=KD), ACT.Copy).then_inc(s_tokC, 1)

            def gelu(e):
                act.wait_ge(s_h, b * NEXP + e + 1)
                act.wait_ge(s_y, b * NEXP + e + 1)
                hold(act)
                for m in range(KD):
                    g = act.activation(hS[:, e % 2, m, :], psH[e % 2][:, m * P:(m + 1) * P], ACT.Gelu, bias=b1_s[:, e, m:m + 1])
                g.then_inc(s_gelu, 1)

            gelu(0)
            gelu(1)
            act.wait_ge(s_gap, b + 1)
            hold(act)
            act.activation(th[:, :], gap[:, :], ACT.Tanh, scale=0.5).then_inc(s_th, 1)
            act.wait_ge(s_combT, b + 1)
            hold(act)
            act.activation(combT[:, :], psT[0:NEXP, 384:512], ACT.Copy).then_inc(s_combC, 1)
            for e in range(2, NEXP):
                gelu(e)
            act.wait_ge(s_yadd, (b + 1) * NEXP + 2)
            hold(act)
            act.dma_start(out[bass.ds(b * P, n), :], res[0:n, :]).then_inc(s_out, 16)

        for l in range(2):
            with act.Fori(0, NI) as i:
                e0, e1 = record(act, i, REC_E, 2, NB)
                if l == 1:
                    e1 = act.snap(e1 - (e1 // NB)).with_bounds(min_val=0, max_val=NB - 1)
                act.wait_ge(s_iter, i + (l * NI + 1))
                hold(act)
                with act.If(e1 > e0):
                    with act.Fori(e0, e1) as b:
                        b = b.with_bounds(min_val=0, max_val=NB - 1 - l)
                        block0(b) if l == 0 else block1(b, P)
        block1(NB - 1, LAST)
        act.wait_ge(s_out, (NB + 1) * 16)

    @block.tensor
    def _(pe):
        pe.sem_inc(s_degmm, 4)
        pe.wait_ge(s_const, 3)
        pe.wait_ge(s_chain, 1 + 7 + 4)
        for n in range(NTR):
            a, c = n // GC, n % GC
            tile = (dst_f, rel_g, ew_g, src_f)[a]
            if n >= 2:
                pe.wait_ge(s_edgeC, n - 1)
            for j in range(GT):
                t = pe.transpose(psH[n % 2][:, j * GQ:(j + 1) * GQ], tile[:, c, j * P:(j + 1) * P], ident[0:GQ, 0:GQ])
            t.then_inc(s_edgeT, 1)
        pe.wait_ge(s_wts, 7 * 16)
        for k in range(KD):
            pe.transpose(psG[:, k * NEXP:(k + 1) * NEXP], rw_s[:, k * P:(k + 1) * P], ident[0:NEXP, 0:NEXP])
        pe.transpose(psG[:, 32:32 + NEXP * KD], b1_r[:, :], ident[0:NEXP * KD, 0:NEXP * KD]).then_inc(s_rwt, 1)
        def deg_mm(j, k, first, last):
            pe.wait_ge(s_onelo, j * 4 + k + 1)
            pe.wait_ge(s_onehi, j * 4 + k + 1)
            pe.matmul(psT[:, 0:NB], onelo[:, k, :], onehi[:, k, :], start=first, stop=last,
                      skip_group_check=True).then_inc(s_degmm, 1)
        for k in range(4):
            deg_mm(0, k, k == 0, False)
        with pe.Fori(1, NT // 4 - 1) as j:
            for k in range(4):
                deg_mm(j, k, False, False)
        for k in range(4):
            deg_mm(NT // 4 - 1, k, False, k == 3)
        with pe.Fori(0, NB // XS) as j:
            for k in range(XS):
                pe.wait_ge(s_y1, j * XS + k + 1)
                pe.wait_ge(s_y1C, j * XS + k + 1)
                hold(pe)
                for m in range(KD):
                    t = pe.transpose(y1banks[k][:, m * P:(m + 1) * P], y1[:, k, m * P:(m + 1) * P], ident[:, :])
                t.then_inc(s_y1T, 1)

        def sums(l, b):
            pe.wait_ge(s_agg[l], b + 1)
            if l == 0:
                pe.wait_ge(s_y2, b + 1)
            else:
                pe.wait_ge(s_b2add, b + 1)
            hold(pe)
            for k in range(KD):
                m = pe.matmul(psG[:, 0:D], aggS[:, k, :], gw[l][:, k, :], start=(k == 0), stop=(k == KD - 1))
            m.then_inc(s_lin[l], 1)

        def block0(b):
            sums(0, b)
            pe.wait_ge(s_y2, b + 2)
            pe.wait_ge(s_y2C, b + 1)
            hold(pe)
            for k in range(KD):
                t = pe.transpose(psT[:, k * P:(k + 1) * P], yS[:, k * P:(k + 1) * P], ident[:, :])
            t.then_inc(s_y2T, 1)

        def block1(b):
            sums(1, b)
            pe.wait_ge(s_tok, b + 1)
            pe.wait_ge(s_combC, b + 1)
            hold(pe)
            for k in range(KD):
                t = pe.transpose(psT[:, k * P:(k + 1) * P], tok[:, k * P:(k + 1) * P], ident[:, :])
            t.then_inc(s_tokT, 1)
            pe.wait_ge(s_tokC, b + 1)
            hold(pe)
            for k in range(KD):
                m = pe.matmul(psT[:, 256:256 + NEXP], tokT[:, k, :], rwT[:, k, :], start=(k == 0), stop=(k == KD - 1))
            m.then_inc(s_lg, 1)

            def hidden(e):
                pe.wait_ge(s_gelu, b * NEXP + e + 1)
                hold(pe)
                for m in range(KD):
                    for k in range(KD):
                        mm = pe.matmul(psH[e % 2][:, m * P:(m + 1) * P], w1_s[:, e, k, m * P:(m + 1) * P], tokT[:, k, :],
                                       start=(k == 0), stop=(k == KD - 1))
                mm.then_inc(s_h, 1)

            def project(e):
                pe.wait_ge(s_gelu, b * NEXP + e + 3)
                pe.wait_ge(s_yadd, b * NEXP + e + 1)
                hold(pe)
                for m in range(KD):
                    mm = pe.matmul(psY[e % 2][:, 0:D], hS[:, e % 2, m, :], w2_s[:, e, m, :], start=(m == 0), stop=(m == KD - 1))
                mm.then_inc(s_y, 1)

            def combine():
                pe.wait_ge(s_comb, b + 1)
                hold(pe)
                pe.transpose(psT[0:NEXP, 384:512], comb[:, :], ident[:, :]).then_inc(s_combT, 1)
                pe.wait_ge(s_combC, b + 2)
                hold(pe)
                pe.matmul(psG[:, 0:D], combT[:, :], b2_s[:, :], start=True, stop=True).then_inc(s_b2, 1)

            hidden(0)
            hidden(1)
            combine()
            for e in range(NEXP):
                project(e)
                if e + 2 < NEXP:
                    hidden(e + 2)

        def group(r, slot, sel_t):
            for h in range(KD):
                for j in range(GT):
                    m = pe.matmul(slot[:, h * W:(h + 1) * W], msg[:, r * GT + j, h * P:(h + 1) * P], sel_t(j),
                                  start=(j == 0), stop=(j == GT - 1))
            return m

        for l in range(2):
            with pe.Fori(0, NI) as i:
                e0, e1 = record(pe, i, REC_E, 2, NB)
                xs = record(pe, i, REC_X, R + 1, NG * (NP // W))
                for r in range(R):
                    g = (i + l * NI) * R + r
                    pe.wait_ge(s_msg[r], (i + l * NI + 1) * (16 * GT))
                    pe.wait_ge(s_sel, g + 1)
                    pe.wait_ge(s_added, g + 1)
                    hold(pe)
                    group(r, part[r % 2], lambda j, r=r: sel[:, r * GT + j, :]).then_inc(s_part, 1)
                with pe.If(xs[R] > xs[0]):
                    for r in range(R):
                        with pe.If(xs[r + 1] > xs[r]):
                            with pe.Fori(xs[r], xs[r + 1]) as n:
                                pe.wait_ge(s_xsel[l], n + 1)
                                hold(pe)
                                group(r, part[0], lambda j: xsel[:, j, :]).then_inc(s_xpart[l], 1)
                        pe.sem_inc(held[pe], 1)
                with pe.If(e1 > e0):
                    with pe.Fori(e0, e1) as b:
                        b = b.with_bounds(min_val=0, max_val=NB - 1)
                        block0(b) if l == 0 else block1(b)

    @block.vector
    def _(v):
        n_chain = [0]

        def link(ins):
            n_chain[0] += 1
            ins.then_inc(s_chain, 1)
            v.wait_ge(s_chain, n_chain[0])

        v.memset(dst_i[:, FULLC, :], N - 1)
        v.memset(src_i[:, FULLC, :], 0)
        v.memset(ew_g[:, FULLC, :], 0.0).then_inc(s_pads, 1)
        for k in range(XS):
            v.memset(xin[:, k, :], 0.0)
        v.memset(xS[:, :], 0.0)
        v.memset(ones_row[:, :], 1.0)
        v.memset(least[:, :, :], BIG)
        v.memset(rec[:, :, :], 0)
        v.memset(xcum[0:1, 0:1], 0.0).then_inc(s_xused, XS)
        v.sem_inc(s_free, R)
        v.sem_inc(s_added, 2)
        v.sem_inc(s_y2, 1)
        v.sem_inc(s_b2add, 1)
        for one in (*s_lin, s_y2T, s_y2C, s_combC):
            v.sem_inc(one, 1)
        for two in (s_gelu, s_yadd, s_y):
            v.sem_inc(two, 2)
        v.wait_ge(s_edges, 9 * 16)
        v.tensor_copy(src_f[:, :, :], src_i[:, :, :])
        link(v.tensor_copy(dst_f[:, :, :], dst_i[:, :, :]))
        v.tensor_reduce(gmax[:, :], dst_f[:, :, :], axis=AX.X, op=ALU.max)
        link(v.tensor_reduce(gmin[:, :], dst_f[:, :, :], axis=AX.X, op=ALU.min))
        link(v.tensor_copy(ints[:, :], gmin[:, :]))
        link(v.tensor_scalar(ints[:, :], ints[:, :], 3, 3, ALU.arith_shift_right, ALU.arith_shift_left))
        link(v.tensor_copy(gbase[:, :], ints[:, :]))
        for c in range(GC):
            link(v.tensor_scalar(rel_g[:, c, :], dst_f[:, c, :], gbase[:, c:c + 1], None, ALU.subtract))
        link(v.tensor_tensor(gextra[:, :], gmax[:, :], gbase[:, :], ALU.subtract))
        link(v.tensor_copy(ints[:, :], gextra[:, :]))
        link(v.tensor_scalar(ints[:, :], ints[:, :], 6, None, ALU.arith_shift_right))
        link(v.tensor_copy(gextra[:, :], ints[:, :]))
        v.sem_inc(s_gout, 3)
        v.wait_ge(s_gready, 16)
        link(v.tensor_tensor_scan(xcum[0:1, 1:NG + 1], ones_row[0:1, :], rows[0:1, 2, :], 0.0, ALU.mult, ALU.add))
        link(v.tensor_reduce(least[0:1, 0, 0:NI], rows[0:1, 0, :].rearrange("o (i r) -> o i r", r=R), axis=AX.X, op=ALU.min))
        a, s = 0, 1
        while s < NI:
            link(v.tensor_tensor(least[0:1, 1 - a, 0:NI], least[0:1, a, 0:NI], least[0:1, a, s:NI + s], ALU.min))
            a, s = 1 - a, 2 * s
        link(v.memset(least[0:1, a, 0:1], 0.0))
        link(v.tensor_scalar(least[0:1, a, 0:NI + 1], least[0:1, a, 0:NI + 1], float(NB * P), None, ALU.min))
        link(v.tensor_copy(eint[:, :], least[0:1, a, 0:NI + 1]))
        link(v.tensor_scalar(eint[:, :], eint[:, :], 7, None, ALU.arith_shift_right))
        for n in range(2):
            v.tensor_copy(rec[0:1, :, REC_E + n], eint[0:1, n:NI + n])
        for n in range(R + 1):
            v.tensor_copy(rec[0:1, :, REC_X + n], xcum[0:1, n:n + R * (NI - 1) + 1:R])
        link(v.tensor_copy(rec[0:1, :, REC_B:REC_B + R], rows[0:1, 1, :].rearrange("o (i r) -> o i r", r=R)))
        v.sem_inc(s_rec, 1)
        v.wait_ge(s_edgeC, NTR)
        link(v.tensor_copy(dst_i32, dstT))
        link(v.tensor_scalar(digit_i, dst_i32, P - 1, None, ALU.bitwise_and))
        link(v.tensor_copy(loT, digit_i))
        link(v.tensor_scalar(digit_i, dst_i32, 7, None, ALU.arith_shift_right))
        link(v.tensor_copy(hiT, digit_i))
        v.sem_inc(s_digits, 1)
        with v.Fori(0, NT // 4) as j:
            for k in range(4):
                v.wait_ge(s_degmm, j * 4 + k + 1)
                v.tensor_scalar(onelo[:, k, :], iota[:, :], loT[:, bass.ds(j * 4 + k, 1)], None, ALU.is_equal).then_inc(s_onelo, 1)

        with v.Fori(0, NB // XS) as j:
            for k in range(XS):
                v.wait_ge(s_xin[k], j * 16 + 16)
                hold(v)
                v.bn_stats(stats[:, k, :], xin[:, k, :]).then_inc(s_xused, 1)
            for k in range(XS):
                v.wait_ge(s_xused, j * XS + (k + 1 + XS))
                hold(v)
                v.bn_aggr(mv7[:, k, :], stats[:, k, :]).then_inc(s_mv, 1)
            v.wait_ge(s_mv, j * (XS + 1) + XS)
            hold(v)
            v.tensor_copy(mv[:, bass.ds(j * XS, XS), :], mv7[:, :, :]).then_inc(s_mv, 1)
        v.wait_ge(s_mv, NB + NB // XS)
        v.wait_ge(s_degmm, NT + 4)
        link(v.tensor_scalar(dinv[:, :], psT[:, 0:NB], 1.0, None, ALU.add))
        link(v.tensor_scalar(lnscale[:, :], mv[:, :, 1], EPS, None, ALU.add))
        v.sem_inc(s_var, 2)
        link(v.memset(accT[:, :, NP:ACCW], 0.0))
        v.wait_ge(s_std, 2)
        link(v.reciprocal(dinv[:, :], dinv[:, :]))
        link(v.reciprocal(lnscale[:, :], lnscale[:, :]))
        link(v.tensor_tensor(lnscale[:, :], lnscale[:, :], dinv[:, :], ALU.mult))
        link(v.tensor_tensor(lnbias[:, :], mv[:, :, 0], lnscale[:, :], ALU.mult))
        link(v.tensor_scalar(lnbias[:, :], lnbias[:, :], -1.0, None, ALU.mult))
        v.sem_inc(s_y1C, XS)

        with v.Fori(0, NB // XS) as j:
            for k in range(XS):
                b = j * XS + k
                v.wait_ge(s_xin[k], j * 16 + (NB // XS + 1) * 16)
                v.wait_ge(s_y1C, b + 1)
                hold(v)
                v.tensor_scalar(y1[:, k, :], xin[:, k, :], lnscale[:, bass.ds(b, 1)], lnbias[:, bass.ds(b, 1)],
                                ALU.mult, ALU.add).then_inc(s_y1, 1)
                v.wait_ge(s_y1, b + 1)
                hold(v)
                v.sem_inc(s_xused, 1)

        def selection(i, r):
            for j in range(GT):
                c = r * GT + j
                t = v.tensor_scalar(sel[:, c, :], iota[:, 0:W], relT[:, bass.ds(i * (R * GT) + c, 1)],
                                    ewT[:, bass.ds(i * (R * GT) + c, 1)], ALU.is_equal, ALU.mult)
            t.then_inc(s_sel, 1)

        def add(g, r, base):
            v.wait_ge(s_part, g + 1)
            v.wait_ge(s_added, g + 2)
            to = accT[:, :, bass.ds(base, W)]
            v.tensor_tensor(to, to, part[r % 2][:, 0:KD * W].rearrange("p (k w) -> p k w", k=KD), ALU.add).then_inc(s_added, 1)

        def further(l, i, r, xs, base):
            v.tensor_copy(xrel[:, :], relT[:, bass.ds(i * (R * GT) + r * GT, GT)])
            v.drain()
            with v.Fori(xs[r], xs[r + 1]) as n:
                v.tensor_scalar(xrel[:, :], xrel[:, :], -float(W), None, ALU.add)
                v.drain()
                for j in range(GT):
                    v.tensor_scalar(xsel[:, j, :], iota[:, 0:W], xrel[:, j:j + 1], ewT[:, bass.ds(i * (R * GT) + r * GT + j, 1)],
                                    ALU.is_equal, ALU.mult)
                v.drain()
                v.sem_inc(s_xsel[l], 1)
                v.wait_ge(s_xpart[l], n + 1)
                hold(v)
                at_col = v.snap(base + (n - xs[r] + 1) * W).with_bounds(min_val=0, max_val=NP)
                to = accT[:, :, bass.ds(at_col, W)]
                v.tensor_tensor(to, to, part[0][:, 0:KD * W].rearrange("p (k w) -> p k w", k=KD), ALU.add)
                v.drain()

        class Chain:

            def __init__(self, s, b):
                self.s, self.b, self.n = s, b, 0

            def __call__(self, ins):
                self.n += 1
                ins.then_inc(self.s, 1)
                v.wait_ge(self.s, self.b * CH + self.n)
                hold(v)

            def end(self):
                assert self.n < CH
                v.sem_inc(self.s, CH - self.n)

        def linear(l, b, then):
            v.wait_ge(s_lin[l], b + 2)
            hold(v)
            then(v.scalar_tensor_tensor(lin[:, :], psG[:, 0:D], dinv[:, bass.ds(b, 1)], gb[l][:, :], ALU.mult, ALU.add))

        def block0(b):
            then = Chain(s_bch[0], b)
            linear(0, b, then)
            v.wait_ge(s_y2out, b * 16 + 16)
            v.wait_ge(s_y2T, b + 1)
            hold(v)
            v.tensor_scalar(yS[:, :], lin[:, :], 0.0, dinv[:, bass.ds(b, 1)], ALU.max, ALU.mult).then_inc(s_y2, 1)
            then.end()

        def block1(b):
            then = Chain(s_bch[1], b)
            linear(1, b, then)
            v.wait_ge(s_x, b * 16 + 16)
            hold(v)
            then(v.scalar_tensor_tensor(x2[:, :], lin[:, :], 0.0, xS[:, :], ALU.max, ALU.add))
            then(v.bn_stats(st1[:, :], x2[:, :]))
            then(v.bn_aggr(mv1[:, :], st1[:, :]))
            then(v.tensor_scalar(var1[:, :], mv1[:, 1:2], EPS, None, ALU.add))
            then(v.tensor_scalar(halfi[:, :], var1[:, :].bitcast(I32), 1, None, ALU.arith_shift_right))
            then(v.tensor_scalar(rs[:, :].bitcast(I32), halfi[:, :], -1.0, float(0x5f3759df), ALU.mult, ALU.add))
            for _ in range(4):
                then(v.tensor_scalar(nt1[:, :], rs[:, :], rs[:, :], var1[:, :], ALU.mult, ALU.mult))
                then(v.tensor_scalar(nt2[:, :], nt1[:, :], -0.5, 1.5, ALU.mult, ALU.add))
                then(v.tensor_tensor(rs[:, :], rs[:, :], nt2[:, :], ALU.mult))
            v.tensor_scalar(tok[:, :], x2[:, :], mv1[:, 0:1], rs[:, :], ALU.subtract, ALU.mult).then_inc(s_tok, 1)
            v.wait_ge(s_tok, b + 1)
            hold(v)
            then(v.tensor_tensor(x2[:, :], x2[:, :], tok[:, :], ALU.add))
            v.wait_ge(s_lg, b + 1)
            hold(v)
            then(v.tensor_copy(lg[:, :], psT[:, 256:256 + NEXP]))
            then(v.max(top[:, :], lg[:, :]))
            v.tensor_tensor(gap[:, :], top[:, 0:1], top[:, 1:2], ALU.subtract).then_inc(s_gap, 1)
            then(v.max_index(topi[:, :], top[:, :], lg[:, :]))
            then(v.tensor_copy(topf[:, :], topi[:, 0:2]))
            v.wait_ge(s_th, b + 1)
            hold(v)
            v.tensor_scalar(wts[:, 0:1], th[:, :], 0.5, 0.5, ALU.mult, ALU.add)
            then(v.tensor_scalar(wts[:, 1:2], th[:, :], -0.5, 0.5, ALU.mult, ALU.add))
            then(v.tensor_scalar(pick[:, :], iota[:, 0:NEXP], topf[:, 0:1], wts[:, 0:1], ALU.is_equal, ALU.mult))
            then(v.tensor_scalar(comb[:, :], iota[:, 0:NEXP], topf[:, 1:2], wts[:, 1:2], ALU.is_equal, ALU.mult))
            v.tensor_tensor(comb[:, :], comb[:, :], pick[:, :], ALU.add).then_inc(s_comb, 1)
            v.wait_ge(s_b2, b + 1)
            v.wait_ge(s_out, b * 16 + 16)
            hold(v)
            v.tensor_tensor(res[:, :], psG[:, 0:D], x2[:, :], ALU.add).then_inc(s_b2add, 1)
            v.wait_ge(s_b2add, b + 2)
            v.wait_ge(s_comb, b + 1)
            for e in range(NEXP):
                v.wait_ge(s_y, b * NEXP + e + 3)
                v.wait_ge(s_yadd, b * NEXP + e + 2)
                hold(v)
                v.scalar_tensor_tensor(res[:, :], psY[e % 2][:, 0:D], comb[:, e:e + 1], res[:, :], ALU.mult, ALU.add)\
                 .then_inc(s_yadd, 1)
            then.end()

        v.wait_ge(s_y2out, 16)
        v.wait_ge(s_out, 16)
        for l in range(2):
            if l == 0:
                v.wait_ge(s_y1C, NB + XS)
            else:
                v.wait_ge(s_y2C, NB + 1)
            with v.Fori(0, NI) as i:
                words = record(v, i, 0, REC, NG * (NP // W))
                e0, e1 = words[0:2]
                xs = words[REC_X:REC_X + R + 1]
                bases = [w.with_bounds(min_val=0, max_val=NP - 8) for w in words[REC_B:REC_B + R]]
                for r in range(R):
                    selection(i, r)
                g0 = (i + l * NI) * R
                with v.If(xs[R] > xs[0]):
                    for r in range(R):
                        add(g0 + r, r, bases[r])
                    v.wait_ge(s_added, g0 + (R + 2))
                    hold(v)
                    for r in range(R):
                        with v.If(xs[r + 1] > xs[r]):
                            further(l, i, r, xs, bases[r])
                        hold(v)
                    v.sem_inc(s_free, R)
                with v.Else():
                    for r in range(R):
                        add(g0 + r, r, bases[r])
                        v.sem_inc(s_free, 1)
                    v.wait_ge(s_added, g0 + (R + 2))
                    hold(v)
                v.sem_inc(s_iter, 1)
                with v.If(e1 > e0):
                    with v.Fori(e0, e1) as b:
                        b = b.with_bounds(min_val=0, max_val=NB - 1)
                        block0(b) if l == 0 else block1(b)

    ctx.close()


_INS = ["x", "src", "dst", "edge_weight", "L0_gnn_W1", "L0_gnn_b1", "L0_gnn_W2", "L0_gnn_b2",
        "L0_ffn_router_w", "L0_ffn_w1", "L0_ffn_b1", "L0_ffn_w2", "L0_ffn_b2"]


def kernel(**inputs):
    import numpy as np
    import concourse.bacc as bacc
    from concourse.bass_utils import run_bass_kernel_spmd

    nc = bacc.Bacc("TRN2", target_bir_lowering=False, num_devices=1)
    arrays, args = {}, []
    for name in _INS:
        a = np.ascontiguousarray(inputs[name])
        arrays[f"in_{name}"] = a
        args.append(nc.dram_tensor(f"in_{name}", a.shape, mybir.dt.from_np(a.dtype), kind="ExternalInput").ap())
    out = nc.dram_tensor("out", [N, D], F32, kind="ExternalOutput").ap()
    build(nc, *args, out)
    r = run_bass_kernel_spmd(nc, [arrays], core_ids=[0])
    return r.results[0]["out"]
```

```python
from contextlib import ExitStack

import concourse.bass as bass
from concourse import mybir

F32 = mybir.dt.float32
I32 = mybir.dt.int32
U32 = mybir.dt.uint32
ALU = mybir.AluOpType
ACT = mybir.ActivationFunctionType
AX = mybir.AxisListType

P = 128
N, D, NEDGE, NEXP = 12500, 256, 200000, 8
KD = D // P
NB = -(-N // P)
NP = NB * P
LAST = N - (NB - 1) * P
GE = 512
GT = GE // P
R = 4
NI = 98
NG = NI * R
NT = NG * GT
W = 128
LO, HI = 16, 8
GQ = 98
GC = NG // GQ
FULLC = NEDGE // (GQ * GE)
REST = NEDGE - FULLC * GQ * GE
RESTQ, RESTE = REST // GE, REST % GE
ACCW = NP + W
REC = 12
REC_E, REC_X, REC_B = 0, 2, 8
EPS = 1e-5
TINY = 1.2e-38
CH = 40
DT = 4
XS = 7
BIG = 1.0e6

assert NG * GE >= NEDGE and FULLC == GC - 1 and R * GT == 16 and LO * HI == W and NI == NB == 2 * XS * (NI // (2 * XS))


def build(nc, x, src, dst, ew, gw1, gb1, gw2, gb2, rw, ew1, eb1, ew2, eb2, out):
    ctx = ExitStack()

    def sb(name, shape, dt=F32):
        return ctx.enter_context(nc.sbuf_tensor(name, shape, dt))

    def pb(name):
        return ctx.enter_context(nc.psum_tensor(name, [P, 512], F32))

    def sem(name):
        return ctx.enter_context(nc.semaphore(name))

    ytab = [nc.dram_tensor(f"ytab{l}", [NP + l * P, D], F32).ap() for l in range(2)]
    gtab = nc.dram_tensor("gtab", [3, NG], F32).ap()

    accbuf = sb("accbuf", [P, KD * ACCW])
    accT = accbuf[:, :].rearrange("p (k n) -> p k n", k=KD)
    at = [0]

    def early(words):
        v = accbuf[:, at[0]:at[0] + words]
        at[0] += words
        return v

    GW = GC * GE
    dst_i = early(GW)[0:GQ, :].bitcast(I32).rearrange("q (c e) -> q c e", c=GC)
    src_i = early(GW)[0:GQ, :].bitcast(I32).rearrange("q (c e) -> q c e", c=GC)
    ew_g = early(GW)[0:GQ, :].rearrange("q (c e) -> q c e", c=GC)
    dst_f = early(GW)[0:GQ, :].rearrange("q (c e) -> q c e", c=GC)
    src_f = early(GW)[0:GQ, :].rearrange("q (c e) -> q c e", c=GC)
    rel_g = early(GW)[0:GQ, :].rearrange("q (c e) -> q c e", c=GC)
    dstT = early(NT)
    digit_i = early(NT).bitcast(I32)
    dst_i32 = early(NT).bitcast(I32)
    loT = early(NT)
    hiT = early(NT)
    rows = early(3 * NG)[0:1, :].rearrange("o (t g) -> o t g", t=3)
    ones_row = early(NG)[0:1, :]
    xcum = early(NG + 1)[0:1, :]
    least = early(2 * (NI + P))[0:1, :].rearrange("o (a n) -> o a n", a=2)
    assert at[0] <= KD * ACCW
    TC = NP // LO + HI
    assert R * TC <= 2 * GW
    degw = accbuf[0:LO, 0:R * TC].rearrange("l (r c) -> l r c", r=R)

    srcT = sb("srcT", [P, NT], I32)
    relT = sb("relT", [P, NT])
    ewT = sb("ewT", [P, NT])
    msg = sb("msg", [P, R * GT, D])
    idx = sb("idx", [P, R * GT], I32)
    sel = sb("sel", [P, R * GT, W])
    xin, y1 = msg[:, 0:XS, :], msg[:, XS:2 * XS, :]
    selw = sel[:, :, :].rearrange("p c w -> p (c w)")
    onelo = selw[:, 0:2 * DT * P].rearrange("p (h k n) -> p h k n", h=2, k=DT)
    onehi = selw[:, 2 * DT * P:2 * DT * (P + NB)].rearrange("p (h k n) -> p h k n", h=2, k=DT)
    wlo = selw[:, 0:2 * R * GT * LO].rearrange("p (h k n) -> p h k n", h=2, k=R * GT)
    whi = selw[:, 2 * R * GT * LO:2 * R * GT * (LO + HI)].rearrange("p (h k n) -> p h k n", h=2, k=R * GT)
    xsel = sb("xsel", [P, GT, W])
    xrel = sb("xrel", [P, GT])
    ident = sb("ident", [P, P])
    iota = sb("iota", [P, P])
    gmin = sb("gmin", [GQ, GC])
    gmax = sb("gmax", [GQ, GC])
    ints = sb("ints", [GQ, GC], I32)
    gbase = sb("gbase", [GQ, GC])
    gextra = sb("gextra", [GQ, GC])
    eint = sb("eint", [1, NI + 1], I32)
    rec = sb("rec", [1, NI, REC], I32)
    dinv = sb("dinv", [P, NB])
    mv = sb("mv", [P, NB, 2])
    mv7 = sb("mv7", [P, XS, 2])
    degT = sb("degT", [NB, P])
    stats = sb("stats", [P, XS, 6])
    lnscale = sb("lnscale", [P, NB])
    lnbias = sb("lnbias", [P, NB])
    gw = [sb(f"gw{l}", [P, KD, D]) for l in range(2)]
    gb = [sb(f"gb{l}", [P, D]) for l in range(2)]
    rwT = sb("rwT", [P, KD, NEXP])
    rw_s = sb("rw_s", [NEXP, D])
    w1_s = sb("w1_s", [P, NEXP, KD, D])
    w2_s = sb("w2_s", [P, NEXP, KD, D])
    b1_s = sb("b1_s", [P, NEXP, KD])
    b1_r = sb("b1_r", [NEXP * KD, P])
    b2_s = sb("b2_s", [NEXP, D])
    aggS = sb("aggS", [P, KD, P])
    lin = sb("lin", [P, D])
    yS = sb("yS", [P, D])
    xS = sb("xS", [P, D])
    x2 = sb("x2", [P, D])
    tok = sb("tok", [P, D])
    tokA = sb("tokA", [P, KD, P])
    tokB = sb("tokB", [P, KD, P])
    front = sb("front", [P, D])
    mix = sb("mix", [P, D])
    res = sb("res", [P, D])
    st1 = sb("st1", [P, 6])
    mv1 = sb("mv1", [P, 2])
    var1 = sb("var1", [P, 1])
    halfi = sb("halfi", [P, 1], I32)
    rs = sb("rs", [P, 1])
    nt1 = sb("nt1", [P, 1])
    nt2 = sb("nt2", [P, 1])
    lg = sb("lg", [P, NEXP])
    top = sb("top", [P, 8])
    topi = sb("topi", [P, 8], U32)
    topf = sb("topf", [P, 2])
    gap = sb("gap", [P, 1])
    th = sb("th", [P, 1])
    wts = sb("wts", [P, 2])
    pick = sb("pick", [P, NEXP])
    comb = sb("comb", [P, NEXP])
    combT = sb("combT", [NEXP, P])
    hS = sb("hS", [P, 2, KD, P])

    part = [pb(f"part{i}") for i in range(2)]
    psG, psT = pb("psG"), pb("psT")
    psH = [pb(f"psH{i}") for i in range(2)]
    psY = [pb(f"psY{i}") for i in range(2)]
    y1banks = [*part, psG, *psH, *psY]

    E = mybir.EngineType
    held = {e: sem(f"held_{n}") for e, n in ((nc.vector, "dve"), (nc.scalar, "act"), (nc.tensor, "pe"), (nc.sync, "sp"), (nc.gpsimd, "pool"))}

    def hold(eng):
        eng.sem_inc(held[eng], 1)

    s_pads = sem("s_pads")
    s_edges = sem("s_edges")
    s_const = sem("s_const")
    s_wts = sem("s_wts")
    s_chain = sem("s_chain")
    s_gout = sem("s_gout")
    s_grow = sem("s_grow")
    s_gready = sem("s_gready")
    s_edgeT = sem("s_edgeT")
    s_edgeC = sem("s_edgeC")
    s_rec = sem("s_rec")
    s_digits = sem("s_digits")
    s_onelo = sem("s_onelo")
    s_onehi = sem("s_onehi")
    s_hieq = sem("s_hieq")
    s_degT = sem("s_degT")
    s_degmm = sem("s_degmm")
    s_wlo = sem("s_wlo")
    s_wheq = sem("s_wheq")
    s_whi = sem("s_whi")
    s_wmm = sem("s_wmm")
    s_wadd = sem("s_wadd")
    s_wsum = sem("s_wsum")
    s_rwt = sem("s_rwt")
    s_xin = [sem(f"s_xin{i}") for i in range(XS)]
    s_xused = sem("s_xused")
    s_mv = sem("s_mv")
    s_std = sem("s_std")
    s_var = sem("s_var")
    s_y1 = sem("s_y1")
    s_y1T = sem("s_y1T")
    s_y1C = sem("s_y1C")
    s_y1out = [sem(f"s_y1out{i}") for i in range(XS)]
    s_msg = [sem(f"s_msg{r}") for r in range(R)]
    s_idx = [sem(f"s_idx{h}") for h in range(2)]
    s_free = sem("s_free")
    s_sel = sem("s_sel")
    s_part = sem("s_part")
    s_added = sem("s_added")
    s_iter = sem("s_iter")
    s_xsel = [sem(f"s_xsel{l}") for l in range(2)]
    s_xpart = [sem(f"s_xpart{l}") for l in range(2)]
    s_xadd = [sem(f"s_xadd{l}") for l in range(2)]
    s_agg = [sem(f"s_agg{l}") for l in range(2)]
    s_lin = [sem(f"s_lin{l}") for l in range(2)]
    s_bch = [sem(f"s_bch{l}") for l in range(2)]
    s_y2 = sem("s_y2")
    s_y2T = sem("s_y2T")
    s_y2C = sem("s_y2C")
    s_y2out = sem("s_y2out")
    s_x = sem("s_x")
    s_tok = sem("s_tok")
    s_tokT = sem("s_tokT")
    s_tokC = sem("s_tokC")
    s_tokB = sem("s_tokB")
    s_linread = sem("s_linread")
    s_lg = sem("s_lg")
    s_gap = sem("s_gap")
    s_th = sem("s_th")
    s_comb = sem("s_comb")
    s_combT = sem("s_combT")
    s_combC = sem("s_combC")
    s_b2 = sem("s_b2")
    s_b2add = sem("s_b2add")
    s_h = sem("s_h")
    s_gelu = sem("s_gelu")
    s_y = sem("s_y")
    s_yadd = sem("s_yadd")
    s_out = sem("s_out")

    block = ctx.enter_context(nc.Block())

    def record(eng, i, at, n, top_value, counted=True):
        _, v = nc.values_load_multi_w_load_instructions(
            rec[0:1, bass.ds(i, 1), at:at + n].rearrange("o i n -> o (i n)"),
            engines=[eng.engine], min_val=0, max_val=top_value,
            skip_runtime_bounds_check_because=None if counted else "they were worked out of node numbers below N, within these bounds")
        return v

    def any_extra(eng):
        return record(eng, NI - 1, REC_X + R, 1, NG * (NP // W), counted=False)[0]

    NTR = 4 * GC

    @block.sync
    def _(sp):
        sp.wait_ge(s_pads, 1)
        for dram, tile in ((dst, dst_i), (src, src_i), (ew, ew_g)):
            sp.dma_start(tile[:, 0:FULLC, :], dram[0:FULLC * GQ * GE].rearrange("(c q e) -> q c e", q=GQ, e=GE)).then_inc(s_edges, 16)
            tail = dram[FULLC * GQ * GE:FULLC * GQ * GE + RESTQ * GE]
            sp.dma_start(tile[0:RESTQ, FULLC, :], tail.rearrange("(q e) -> q e", e=GE)).then_inc(s_edges, 16)
            sp.dma_start(tile[RESTQ:RESTQ + 1, FULLC, 0:RESTE], dram[NEDGE - RESTE:NEDGE].rearrange("(a e) -> a e", a=1)).then_inc(s_edges, 16)
        sp.wait_ge(s_gout, 3)
        with nc.allow_non_contiguous_dma(reason="784 words, once"):
            for n, t in enumerate((gmin, gbase, gextra)):
                sp.dma_start(gtab[n, :].rearrange("(c q) -> q c", q=GQ), t[:, :]).then_inc(s_grow, 16)
        sp.wait_ge(s_grow, 48)
        sp.dma_start(rows[:, :, :], gtab.rearrange("(o t) g -> o t g", o=1)).then_inc(s_gready, 16)
        def load_x(turn, j, k, n):
            sp.wait_ge(s_xused, (j + turn * (NB // XS)) * XS + k + 1)
            hold(sp)
            sp.dma_start(xin[0:n, k, :], x[bass.ds(j * (XS * P) + k * P, n), :]).then_inc(s_xin[k], 16)

        def store_y1(j, k):
            sp.wait_ge(s_y1, j * XS + k + 1)
            hold(sp)
            sp.dma_start(ytab[0][bass.ds(j * (XS * P) + k * P, P), :], y1[:, k, :]).then_inc(s_y1out[k], 16)

        with sp.Fori(0, NB // XS - 1) as j:
            for k in range(XS):
                load_x(0, j, k, P)
        for k in range(XS):
            load_x(0, NB // XS - 1, k, P if k < XS - 1 else LAST)
        for k in range(XS):
            load_x(1, 0, k, P)
        def turn(j, rows_of_last):
            for k in range(XS):
                store_y1(j - 1, k)
            for k in range(XS):
                sp.wait_ge(s_y1out[k], j * 16)
                hold(sp)
                load_x(1, j, k, P if k < XS - 1 else rows_of_last)

        with sp.Fori(1, NB // XS - 1) as j:
            turn(j, P)
        turn(NB // XS - 1, LAST)
        for k in range(XS):
            store_y1(NB // XS - 1, k)
        HC = R * GT // 2

        def stage(l, i, first):
            for h in range(2):
                if not first:
                    for r in range(R // 2):
                        sp.wait_ge(s_msg[h * R // 2 + r], (i + l * NI) * (16 * GT))
                        hold(sp)
                sp.dma_start(idx[:, h * HC:(h + 1) * HC], srcT[:, bass.ds(i * (2 * HC) + h * HC, HC)]).then_inc(s_idx[h], 16)

        sp.wait_ge(s_edgeC, NTR)
        stage(0, 0, True)
        with sp.Fori(1, NI) as i:
            stage(0, i, False)
        with sp.Fori(0, NI) as i:
            stage(1, i, False)

    @block.gpsimd
    def _(pool):
        pool.memset(ident[:, :], 0.0).then_inc(s_const, 1)
        pool.iota(iota[:, :], [[1, P]], base=0, channel_multiplier=0, allow_small_or_imprecise_dtypes=True).then_inc(s_const, 1)
        pool.wait_ge(s_const, 2)
        pool.affine_select(out=ident[:, :], in_=ident[:, :], compare_op=ALU.not_equal, fill=1.0, base=0,
                           pattern=[[-1, P]], channel_multiplier=1).then_inc(s_const, 1)
        pool.wait_ge(s_digits, 1)
        with pool.If(any_extra(pool) > 0):
            with pool.Fori(0, NT // (2 * DT)) as j:
                for h in range(2):
                    pool.wait_ge(s_hieq, j * 2 + h + 1)
                    hold(pool)
                    pool.tensor_tensor(onehi[:, h, :, :], onehi[:, h, :, :],
                                       ewT[:, bass.ds((j * 2 + h) * DT, DT)].unsqueeze(2).broadcast_to([P, DT, NB]), ALU.mult)\
                        .then_inc(s_onehi, 1)
        with pool.Else():
            with pool.Fori(0, NI // 2) as j:
                for h in range(2):
                    pool.wait_ge(s_wheq, j * 2 + h + 1)
                    hold(pool)
                    pool.tensor_tensor(whi[:, h, :, :], whi[:, h, :, :],
                                       ewT[:, bass.ds((j * 2 + h) * R * GT, R * GT)].unsqueeze(2).broadcast_to([P, R * GT, HI]),
                                       ALU.mult).then_inc(s_whi, 1)
        for l in range(2):
            if l == 0:
                for k in range(XS):
                    pool.wait_ge(s_y1out[k], NB // XS * 16)
                pool.wait_ge(s_y1C, NB + XS)
            else:
                pool.wait_ge(s_y2out, (NB + 2) * 16)
            with pool.Fori(0, NI) as i:
                for r in range(R):
                    pool.wait_ge(s_free, (i + l * NI) * R + r + 1)
                    hold(pool)
                    if r % (R // 2) == 0:
                        pool.wait_ge(s_idx[r // (R // 2)], (i + l * NI) * 16 + 16)
                        hold(pool)
                    for j in range(GT):
                        c = r * GT + j
                        pool.indirect_dma_start(msg[:, c, :], None, ytab[l], bass.IndirectOffsetOnAxis(
                            ap=idx[:, c:c + 1].bitcast(U32), axis=0)).then_inc(s_msg[r], 16)

    @block.scalar
    def _(act):
        for l, (w, b) in enumerate(((gw1, gb1), (gw2, gb2))):
            act.dma_start(gw[l][:, :, :], w.rearrange("(k p) n -> p k n", p=P)).then_inc(s_wts, 16)
            act.dma_start(gb[l][:, :], b.rearrange("(o n) -> o n", o=1).broadcast_to([P, D])).then_inc((s_y2out, s_out)[l], 16)
        act.dma_start(rw_s[:, :], rw).then_inc(s_wts, 16)
        act.dma_start(b1_r[:, :], eb1.rearrange("e (k p) -> (e k) p", p=P)).then_inc(s_wts, 16)
        act.dma_start(b2_s[:, :], eb2).then_inc(s_wts, 16)
        act.dma_start(w1_s[:, :, :, :], ew1.rearrange("e (k p) n -> p e k n", p=P)).then_inc(s_wts, 16)
        act.dma_start(w2_s[:, :, :, :], ew2.rearrange("e (k p) n -> p e k n", p=P)).then_inc(s_wts, 16)
        for n in range(NTR):
            a, c = n // GC, n % GC
            tile = (dstT, relT, ewT, srcT)[a]
            act.wait_ge(s_edgeT, n + 1)
            act.activation(tile[:, c * GQ * GT:(c + 1) * GQ * GT].rearrange("p (q j) -> p j q", j=GT),
                           (psH[n % 2])[:, 0:GT * GQ].rearrange("p (j q) -> p j q", j=GT), ACT.Copy).then_inc(s_edgeC, 1)
        act.wait_ge(s_rwt, 1)
        act.activation(rwT[:, :, :].rearrange("p k e -> p (k e)"), psG[:, 0:KD * NEXP], ACT.Copy).then_inc(s_rwt, 1)
        act.activation(b1_s[:, :, :].rearrange("p e k -> p (e k)"), psG[:, 32:32 + NEXP * KD], ACT.Copy).then_inc(s_rwt, 1)
        act.wait_ge(s_var, 2)
        act.activation(dinv[:, :], dinv[:, :], ACT.Sqrt).then_inc(s_std, 1)
        act.activation(lnscale[:, :], lnscale[:, :], ACT.Sqrt).then_inc(s_std, 1)
        act.preload_act_table(ACT.Gelu)
        with act.Fori(0, NB // XS) as j:
            for k in range(XS):
                act.wait_ge(s_y1T, j * XS + k + 1)
                hold(act)
                act.activation(accT[:, :, bass.ds(j * (XS * P) + k * P, P)],
                               y1banks[k][:, 0:D].rearrange("p (k n) -> p k n", k=KD), ACT.Copy).then_inc(s_y1C, 1)

        def sums(l, b):
            act.wait_ge(s_lin[l], b + 1)
            hold(act)
            act.activation(aggS[:, :, :], accT[:, :, bass.ds(b * P, P)], ACT.Copy).then_inc(s_agg[l], 1)

        def behind(b):
            return (b + NB) % (NB + 1) if not isinstance(b, int) else b - 1

        def store0(b):
            act.wait_ge(s_y2, b + 1)
            hold(act)
            act.dma_start(ytab[1][bass.ds(behind(b) * P, P), :], yS[:, :]).then_inc(s_y2out, 16)
            act.wait_ge(s_y2T, b + 2)
            act.wait_ge(s_agg[0], b + (1 if not isinstance(b, int) else 0))
            hold(act)
            act.activation(accT[:, :, bass.ds(behind(b) * P, P)], psT[:, 0:D].rearrange("p (k n) -> p k n", k=KD),
                           ACT.Copy).then_inc(s_y2C, 1)

        def block0(b):
            sums(0, b)
            store0(b)

        def block1(b, ahead=True):
            if ahead:
                sums(1, b)
            act.wait_ge(s_gap, b + 1)
            hold(act)
            act.activation(th[:, :], gap[:, :], ACT.Tanh, scale=0.5).then_inc(s_th, 1)
            act.wait_ge(s_yadd, b * NEXP + 2)
            hold(act)
            row = (b - 2) * P if isinstance(b, int) else act.snap((b + NB - 3) % (NB - 1) * P).with_bounds(min_val=0, max_val=(NB - 2) * P)
            act.dma_start(out[bass.ds(row, P), :], res[:, :]).then_inc(s_out, 16)
            if ahead:
                act.wait_ge(s_tok, b + 1)
                hold(act)
                with act.If(b < NB - 1):
                    whole = b.with_bounds(max_val=NB - 2)
                    act.dma_start(xS[:, :], x[bass.ds(whole * P, P), :]).then_inc(s_x, 16)
                with act.Else():
                    act.dma_start(xS[0:LAST, :], x[(NB - 1) * P:N, :]).then_inc(s_x, 16)

            def gelu(e):
                act.wait_ge(s_h, b * NEXP + e + 2)
                act.wait_ge(s_y, b * NEXP + e + 1)
                hold(act)
                for m in range(KD):
                    g = act.activation(hS[:, e % 2, m, :], psH[e % 2][:, m * P:(m + 1) * P], ACT.Gelu, bias=b1_s[:, e, m:m + 1])
                g.then_inc(s_gelu, 1)

            for e in range(3):
                gelu(e)
            act.wait_ge(s_combT, b + 1)
            act.wait_ge(s_b2, b + 1)
            hold(act)
            act.activation(combT[:, :], psT[0:NEXP, 384:512], ACT.Copy).then_inc(s_combC, 1)
            for e in range(3, NEXP - 1):
                gelu(e)
            if ahead:
                act.wait_ge(s_tokT, b + 1)
                act.wait_ge(s_tokB, b + 1)
                hold(act)
                act.activation(tokA[:, :, :], psT[:, 0:D].rearrange("p (k n) -> p k n", k=KD), ACT.Copy).then_inc(s_tokC, 1)
            gelu(NEXP - 1)
            if ahead:
                act.wait_ge(s_h, b * NEXP + NEXP + 1)
                act.wait_ge(s_tokC, b + 1)
                hold(act)
                act.activation(tokB[:, :, :], tokA[:, :, :], ACT.Copy).then_inc(s_tokB, 1)

        for l in range(2):
            body = (block0, block1)[l]
            with act.Fori(0, NI) as i:
                e0, e1 = record(act, i, REC_E, 2, NB)
                with act.If(e1 > e0):
                    act.wait_ge(s_iter, i + l * NI)
                    hold(act)
                    with act.Fori(e0, e1) as b:
                        body(b.with_bounds(min_val=0, max_val=NB - 1))
            e0 = record(act, NI - 1, REC_E + 1, 1, NB - 1)[0]
            act.wait_ge(s_iter, (l + 1) * NI)
            with act.Fori(e0, NB) as b:
                body(b.with_bounds(min_val=0, max_val=NB - 1))
            store0(NB) if l == 0 else block1(NB, ahead=False)
        act.wait_ge(s_yadd, (NB + 1) * NEXP + 2)
        act.dma_start(out[(NB - 1) * P:N, :], res[0:LAST, :]).then_inc(s_out, 16)
        act.wait_ge(s_out, (NB + 3) * 16)

    @block.tensor
    def _(pe):
        pe.sem_inc(s_degmm, 2)
        pe.wait_ge(s_const, 3)
        pe.wait_ge(s_chain, 1 + 7 + 4)
        for n in range(NTR):
            a, c = n // GC, n % GC
            tile = (dst_f, rel_g, ew_g, src_f)[a]
            if n >= 2:
                pe.wait_ge(s_edgeC, n - 1)
            for j in range(GT):
                t = pe.transpose(psH[n % 2][:, j * GQ:(j + 1) * GQ], tile[:, c, j * P:(j + 1) * P], ident[0:GQ, 0:GQ])
            t.then_inc(s_edgeT, 1)
        pe.wait_ge(s_wts, 7 * 16)
        for k in range(KD):
            pe.transpose(psG[:, k * NEXP:(k + 1) * NEXP], rw_s[:, k * P:(k + 1) * P], ident[0:NEXP, 0:NEXP])
        pe.transpose(psG[:, 32:32 + NEXP * KD], b1_r[:, :], ident[0:NEXP * KD, 0:NEXP * KD]).then_inc(s_rwt, 1)
        def deg_step(j, h, first, last):
            pe.wait_ge(s_onelo, j * 2 + h + 1)
            pe.wait_ge(s_onehi, j * 2 + h + 1)
            for k in range(DT):
                m = pe.matmul(psT[0:NB, 0:P], onehi[:, h, k, :], onelo[:, h, k, :], start=first and k == 0,
                              stop=last and k == DT - 1, skip_group_check=True)
            m.then_inc(s_degmm, 1)
        pe.wait_ge(s_digits, 1)
        with pe.If(any_extra(pe) > 0):
            for h in range(2):
                deg_step(0, h, h == 0, False)
            with pe.Fori(1, NT // (2 * DT) - 1) as j:
                for h in range(2):
                    deg_step(j, h, False, False)
            for h in range(2):
                deg_step(NT // (2 * DT) - 1, h, False, h == 1)
        with pe.Else():
            with pe.Fori(0, NI // 2) as j:
                for h in range(2):
                    pe.wait_ge(s_wlo, j * 2 + h + 1)
                    pe.wait_ge(s_whi, j * 2 + h + 1)
                    hold(pe)
                    for r in range(R):
                        for k in range(GT):
                            m = pe.matmul(part[h][0:LO, r * HI:(r + 1) * HI], wlo[:, h, r * GT + k, :], whi[:, h, r * GT + k, :],
                                          start=(k == 0), stop=(k == GT - 1))
                    m.then_inc(s_wmm, 1)
            pe.wait_ge(s_wsum, 1)
            for k in range(P // LO):
                t = pe.transpose(psT[0:NB, k * LO:(k + 1) * LO], degw[:, 0, k:NP // LO:P // LO], ident[0:LO, 0:LO])
            t.then_inc(s_wsum, 1)
        pe.wait_ge(s_degT, 1)
        pe.transpose(psT[:, 128:128 + NB], degT[:, :], ident[0:NB, 0:NB]).then_inc(s_degT, 1)
        with pe.Fori(0, NB // XS) as j:
            for k in range(XS):
                pe.wait_ge(s_y1, j * XS + k + 1)
                pe.wait_ge(s_y1C, j * XS + k + 1)
                hold(pe)
                for m in range(KD):
                    t = pe.transpose(y1banks[k][:, m * P:(m + 1) * P], y1[:, k, m * P:(m + 1) * P], ident[:, :])
                t.then_inc(s_y1T, 1)

        def sums(l, b):
            pe.wait_ge(s_agg[l], b + 1)
            if l == 0:
                pe.wait_ge(s_y2, b + 1)
            else:
                pe.wait_ge(s_b2add, b + 1)
            hold(pe)
            for k in range(KD):
                m = pe.matmul(psG[:, 0:D], aggS[:, k, :], gw[l][:, k, :], start=(k == 0), stop=(k == KD - 1))
            m.then_inc(s_lin[l], 1)

        def turn0(b):
            pe.wait_ge(s_y2, b + 1)
            pe.wait_ge(s_y2C, b + 1)
            hold(pe)
            for k in range(KD):
                t = pe.transpose(psT[:, k * P:(k + 1) * P], yS[:, k * P:(k + 1) * P], ident[:, :])
            t.then_inc(s_y2T, 1)

        def block0(b):
            sums(0, b)
            turn0(b)

        def block1(b, ahead=True):
            pe.wait_ge(s_tokB, b + 1)

            def hidden(e):
                pe.wait_ge(s_gelu, b * NEXP + e + 1)
                hold(pe)
                for m in range(KD):
                    for k in range(KD):
                        mm = pe.matmul(psH[e % 2][:, m * P:(m + 1) * P], w1_s[:, e, k, m * P:(m + 1) * P], tokB[:, k, :],
                                       start=(k == 0), stop=(k == KD - 1))
                mm.then_inc(s_h, 1)

            def project(e):
                pe.wait_ge(s_gelu, b * NEXP + e + 3)
                pe.wait_ge(s_yadd, b * NEXP + e + 1)
                hold(pe)
                for m in range(KD):
                    mm = pe.matmul(psY[e % 2][:, 0:D], hS[:, e % 2, m, :], w2_s[:, e, m, :], start=(m == 0), stop=(m == KD - 1))
                mm.then_inc(s_y, 1)

            hidden(0)
            if ahead:
                sums(1, b)
            hidden(1)
            project(0)
            hidden(2)
            pe.wait_ge(s_comb, b + 1)
            pe.wait_ge(s_gap, b + 1)
            hold(pe)
            pe.transpose(psT[0:NEXP, 384:512], comb[:, :], ident[:, :]).then_inc(s_combT, 1)
            project(1)
            hidden(3)
            project(2)
            hidden(4)
            project(3)
            hidden(5)
            pe.wait_ge(s_combC, b + 1)
            if ahead:
                pe.wait_ge(s_linread, b + 1)
            hold(pe)
            pe.matmul(psG[:, 0:D], combT[:, :], b2_s[:, :], start=True, stop=True).then_inc(s_b2, 1)
            project(4)
            hidden(6)
            project(5)
            if ahead:
                pe.wait_ge(s_tok, b + 2)
                hold(pe)
                for k in range(KD):
                    t = pe.transpose(psT[:, k * P:(k + 1) * P], tok[:, k * P:(k + 1) * P], ident[:, :])
                t.then_inc(s_tokT, 1)
            hidden(7)
            project(6)
            if ahead:
                pe.wait_ge(s_tokC, b + 1)
                hold(pe)
                for k in range(KD):
                    m = pe.matmul(psT[:, 256:256 + NEXP], tokA[:, k, :], rwT[:, k, :], start=(k == 0), stop=(k == KD - 1))
                m.then_inc(s_lg, 1)
            project(7)

        def group(r, slot, sel_t):
            for h in range(KD):
                for j in range(GT):
                    m = pe.matmul(slot[:, h * W:(h + 1) * W], msg[:, r * GT + j, h * P:(h + 1) * P], sel_t(j),
                                  start=(j == 0), stop=(j == GT - 1))
            return m

        for l in range(2):
            body = (block0, block1)[l]
            with pe.Fori(0, NI) as i:
                for r in range(R):
                    g = (i + l * NI) * R + r
                    pe.wait_ge(s_msg[r], (i + l * NI + 1) * (16 * GT))
                    pe.wait_ge(s_sel, g + 1)
                    pe.wait_ge(s_added, g + 1)
                    hold(pe)
                    group(r, part[r % 2], lambda j, r=r: sel[:, r * GT + j, :]).then_inc(s_part, 1)
                e0, e1 = record(pe, i, REC_E, 2, NB)
                xs = record(pe, i, REC_X, R + 1, NG * (NP // W), counted=False)
                with pe.If(xs[R] > xs[0]):
                    xs = record(pe, i, REC_X, R + 1, NG * (NP // W))
                    for r in range(R):
                        with pe.If(xs[r + 1] > xs[r]):
                            with pe.Fori(xs[r], xs[r + 1]) as n:
                                pe.wait_ge(s_xsel[l], n + 1)
                                hold(pe)
                                group(r, part[0], lambda j: xsel[:, j, :]).then_inc(s_xpart[l], 1)
                        pe.sem_inc(held[pe], 1)
                with pe.If(e1 > e0):
                    with pe.Fori(e0, e1) as b:
                        body(b.with_bounds(min_val=0, max_val=NB - 1))
            with pe.Fori(record(pe, NI - 1, REC_E + 1, 1, NB - 1)[0], NB) as b:
                body(b.with_bounds(min_val=0, max_val=NB - 1))
            turn0(NB) if l == 0 else block1(NB, ahead=False)

    @block.vector
    def _(v):
        n_chain = [0]

        def link(ins):
            n_chain[0] += 1
            ins.then_inc(s_chain, 1)
            v.wait_ge(s_chain, n_chain[0])

        v.memset(dst_i[:, FULLC, :], N - 1)
        v.memset(src_i[:, FULLC, :], 0)
        v.memset(ew_g[:, FULLC, :], 0.0).then_inc(s_pads, 1)
        for k in range(XS):
            v.memset(xin[:, k, :], 0.0)
        for t in (xS, yS, res, front, gap):
            v.memset(t[:, :], 0.0)
        v.memset(tokB[:, :, :], 0.0)
        v.memset(topi[:, :], 0)
        v.memset(ones_row[:, :], 1.0)
        v.memset(least[:, :, :], BIG)
        v.memset(rec[:, :, :], 0)
        v.memset(xcum[0:1, 0:1], 0.0).then_inc(s_xused, XS)
        v.sem_inc(s_free, R)
        v.sem_inc(s_added, 2)
        v.sem_inc(s_y2, 1)
        v.sem_inc(s_b2add, 1)
        for one in (*s_lin, s_y2T, s_y2C, s_h, s_gap, s_tok, s_tokB, s_b2):
            v.sem_inc(one, 1)
        for two in (s_gelu, s_yadd, s_y):
            v.sem_inc(two, 2)
        v.wait_ge(s_edges, 9 * 16)
        v.tensor_copy(src_f[:, :, :], src_i[:, :, :])
        link(v.tensor_copy(dst_f[:, :, :], dst_i[:, :, :]))
        v.tensor_reduce(gmax[:, :], dst_f[:, :, :], axis=AX.X, op=ALU.max)
        link(v.tensor_reduce(gmin[:, :], dst_f[:, :, :], axis=AX.X, op=ALU.min))
        link(v.tensor_copy(ints[:, :], gmin[:, :]))
        link(v.tensor_scalar(ints[:, :], ints[:, :], 4, 4, ALU.arith_shift_right, ALU.arith_shift_left))
        link(v.tensor_copy(gbase[:, :], ints[:, :]))
        for c in range(GC):
            link(v.tensor_scalar(rel_g[:, c, :], dst_f[:, c, :], gbase[:, c:c + 1], None, ALU.subtract))
        link(v.tensor_tensor(gextra[:, :], gmax[:, :], gbase[:, :], ALU.subtract))
        link(v.tensor_copy(ints[:, :], gextra[:, :]))
        link(v.tensor_scalar(ints[:, :], ints[:, :], W.bit_length() - 1, None, ALU.arith_shift_right))
        link(v.tensor_copy(gextra[:, :], ints[:, :]))
        v.sem_inc(s_gout, 3)
        v.wait_ge(s_gready, 16)
        link(v.tensor_tensor_scan(xcum[0:1, 1:NG + 1], ones_row[0:1, :], rows[0:1, 2, :], 0.0, ALU.mult, ALU.add))
        link(v.tensor_reduce(least[0:1, 0, 0:NI], rows[0:1, 0, :].rearrange("o (i r) -> o i r", r=R), axis=AX.X, op=ALU.min))
        a, s = 0, 1
        while s < NI:
            link(v.tensor_tensor(least[0:1, 1 - a, 0:NI], least[0:1, a, 0:NI], least[0:1, a, s:NI + s], ALU.min))
            a, s = 1 - a, 2 * s
        link(v.memset(least[0:1, a, 0:1], 0.0))
        link(v.tensor_scalar(least[0:1, a, 0:NI + 1], least[0:1, a, 0:NI + 1], float(NB * P), None, ALU.min))
        link(v.tensor_copy(eint[:, :], least[0:1, a, 0:NI + 1]))
        link(v.tensor_scalar(eint[:, :], eint[:, :], 7, None, ALU.arith_shift_right))
        v.tensor_copy(rec[0:1, 1:NI, REC_E], eint[0:1, 0:NI - 1])
        v.tensor_copy(rec[0:1, :, REC_E + 1], eint[0:1, 0:NI])
        for n in range(R + 1):
            v.tensor_copy(rec[0:1, :, REC_X + n], xcum[0:1, n:n + R * (NI - 1) + 1:R])
        link(v.tensor_copy(rec[0:1, :, REC_B:REC_B + R], rows[0:1, 1, :].rearrange("o (i r) -> o i r", r=R)))
        v.sem_inc(s_rec, 1)
        v.wait_ge(s_edgeC, NTR)

        def digits(numbers, low):
            link(v.tensor_copy(dst_i32, numbers))
            link(v.tensor_scalar(digit_i, dst_i32, 2 ** low - 1, None, ALU.bitwise_and))
            link(v.tensor_copy(loT, digit_i))
            link(v.tensor_scalar(digit_i, dst_i32, low, None, ALU.arith_shift_right))
            link(v.tensor_copy(hiT, digit_i))
            v.sem_inc(s_digits, 1)

        def one_hot(out, n, digit, t, tiles):
            return v.tensor_tensor(out, iota[:, 0:n].unsqueeze(1).broadcast_to([P, tiles, n]),
                                   digit[:, bass.ds(t, tiles)].unsqueeze(2).broadcast_to([P, tiles, n]), ALU.is_equal)

        def statistics(q, k):
            v.wait_ge(s_xin[k], q * 16 + 16)
            hold(v)
            v.bn_stats(stats[:, k, :], xin[:, k, :]).then_inc(s_xused, 1)

        def end_turn(q):
            for k in range(XS):
                v.wait_ge(s_xused, q * XS + (k + 1 + XS))
                hold(v)
                v.bn_aggr(mv7[:, k, :], stats[:, k, :]).then_inc(s_mv, 1)
            v.wait_ge(s_mv, q * (XS + 1) + XS)
            hold(v)
            v.tensor_copy(mv[:, bass.ds(q * XS, XS), :], mv7[:, :, :]).then_inc(s_mv, 1)

        links_before = n_chain[0]
        with v.If(any_extra(v) > 0):
            digits(dstT, P.bit_length() - 1)
            with v.Fori(0, NT // (2 * DT)) as j:
                for h in range(2):
                    v.wait_ge(s_degmm, j * 2 + h + 1)
                    one_hot(onehi[:, h, :, :], NB, hiT, (j * 2 + h) * DT, DT).then_inc(s_hieq, 1)
                    one_hot(onelo[:, h, :, :], P, loT, (j * 2 + h) * DT, DT).then_inc(s_onelo, 1)
            v.wait_ge(s_degmm, NT // DT + 2)
            with v.Fori(0, NB // XS) as j:
                for k in range(XS):
                    statistics(j, k)
                end_turn(j)
        with v.Else():
            n_chain[0] = links_before
            digits(relT[:, :], LO.bit_length() - 1)

            def window_digits(i, h):
                one_hot(whi[:, h, :, :], HI, hiT, i * (R * GT), R * GT).then_inc(s_wheq, 1)
                one_hot(wlo[:, h, :, :], LO, loT, i * (R * GT), R * GT).then_inc(s_wlo, 1)

            def window_adds(i, h):
                bases = record(v, i, REC_B, R, NP - LO, counted=False)
                v.wait_ge(s_wmm, i + 1)
                v.wait_ge(s_wadd, i + 1)
                hold(v)
                for r in range(R):
                    to = degw[:, r, bass.ds(bases[r] // LO, HI)]
                    t = v.tensor_tensor(to, to, part[h][0:LO, r * HI:(r + 1) * HI], ALU.add)
                t.then_inc(s_wadd, 1)

            v.memset(degw[:, :, :], 0.0).then_inc(s_wadd, 1)
            for h in range(2):
                window_digits(h, h)
            with v.Fori(0, NI // (2 * XS)) as j:
                for u in range(2 * XS):
                    i = j * (2 * XS) + u
                    window_adds(i, u % 2)
                    window_digits(v.snap((i + 2) % NI), u % 2)
                    statistics(j * 2 + u // XS, u % XS)
                    if u % XS == XS - 1:
                        end_turn(j * 2 + u // XS)
            v.wait_ge(s_wadd, NI + 1)
            v.tensor_tensor(degw[:, 0:2, :], degw[:, 0:2, :], degw[:, 2:4, :], ALU.add).then_inc(s_wadd, 1)
            v.wait_ge(s_wadd, NI + 2)
            v.tensor_tensor(degw[:, 0, :], degw[:, 0, :], degw[:, 1, :], ALU.add).then_inc(s_wsum, 1)
            v.wait_ge(s_wsum, 2)

        v.wait_ge(s_mv, NB + NB // XS)
        link(v.tensor_scalar(degT[:, :], psT[0:NB, 0:P], 1.0, None, ALU.add))
        v.sem_inc(s_degT, 1)
        v.wait_ge(s_degT, 2)
        link(v.tensor_scalar(lnbias[:, :], psT[:, 128:128 + NB], 0.0, None, ALU.is_gt))
        link(v.tensor_scalar(dinv[:, :], psT[:, 128:128 + NB], TINY, None, ALU.max))
        link(v.tensor_scalar(lnscale[:, :], mv[:, :, 1], EPS, None, ALU.add))
        v.sem_inc(s_var, 2)
        link(v.memset(accT[:, :, NP:ACCW], 0.0))
        v.wait_ge(s_std, 2)
        link(v.reciprocal(dinv[:, :], dinv[:, :]))
        link(v.tensor_tensor(dinv[:, :], dinv[:, :], lnbias[:, :], ALU.mult))
        link(v.reciprocal(lnscale[:, :], lnscale[:, :]))
        link(v.tensor_tensor(lnscale[:, :], lnscale[:, :], dinv[:, :], ALU.mult))
        link(v.tensor_tensor(lnbias[:, :], mv[:, :, 0], lnscale[:, :], ALU.mult))
        link(v.tensor_scalar(lnbias[:, :], lnbias[:, :], -1.0, None, ALU.mult))
        v.sem_inc(s_y1C, XS)

        with v.Fori(0, NB // XS) as j:
            for k in range(XS):
                b = j * XS + k
                v.wait_ge(s_xin[k], j * 16 + (NB // XS + 1) * 16)
                v.wait_ge(s_y1C, b + 1)
                hold(v)
                v.tensor_scalar(y1[:, k, :], xin[:, k, :], lnscale[:, bass.ds(b, 1)], lnbias[:, bass.ds(b, 1)],
                                ALU.mult, ALU.add).then_inc(s_y1, 1)
                v.wait_ge(s_y1, b + 1)
                hold(v)
                v.sem_inc(s_xused, 1)

        def selection(i, r):
            for j in range(GT):
                c = r * GT + j
                t = v.tensor_scalar(sel[:, c, :], iota[:, 0:W], relT[:, bass.ds(i * (R * GT) + c, 1)],
                                    ewT[:, bass.ds(i * (R * GT) + c, 1)], ALU.is_equal, ALU.mult)
            t.then_inc(s_sel, 1)

        def add(g, r, base):
            v.wait_ge(s_part, g + 1)
            v.wait_ge(s_added, g + 2)
            to = accT[:, :, bass.ds(base, W)]
            v.tensor_tensor(to, to, part[r % 2][:, 0:KD * W].rearrange("p (k w) -> p k w", k=KD), ALU.add).then_inc(s_added, 1)

        def further(l, i, r, xs, base):
            v.tensor_copy(xrel[:, :], relT[:, bass.ds(i * (R * GT) + r * GT, GT)])
            v.drain()
            with v.Fori(xs[r], xs[r + 1]) as n:
                v.tensor_scalar(xrel[:, :], xrel[:, :], -float(W), None, ALU.add)
                v.drain()
                for j in range(GT):
                    v.tensor_scalar(xsel[:, j, :], iota[:, 0:W], xrel[:, j:j + 1], ewT[:, bass.ds(i * (R * GT) + r * GT + j, 1)],
                                    ALU.is_equal, ALU.mult)
                v.drain()
                v.sem_inc(s_xsel[l], 1)
                v.wait_ge(s_xpart[l], n + 1)
                hold(v)
                at_col = v.snap(base + (n - xs[r] + 1) * W).with_bounds(min_val=0, max_val=NP)
                to = accT[:, :, bass.ds(at_col, W)]
                v.tensor_tensor(to, to, part[0][:, 0:KD * W].rearrange("p (k w) -> p k w", k=KD), ALU.add)
                v.drain()

        class Chain:

            def __init__(self, s, b):
                self.s, self.b, self.n = s, b, 0

            def __call__(self, ins):
                self.n += 1
                ins.then_inc(self.s, 1)
                v.wait_ge(self.s, self.b * CH + self.n)
                hold(v)

            def end(self):
                assert self.n < CH
                v.sem_inc(self.s, CH - self.n)

        def linear(l, b, then):
            v.wait_ge(s_lin[l], b + 2)
            hold(v)
            then(v.scalar_tensor_tensor(lin[:, :], psG[:, 0:D], dinv[:, bass.ds(b, 1)], gb[l][:, :], ALU.mult, ALU.add))

        def block0(b):
            then = Chain(s_bch[0], b)
            linear(0, b, then)
            v.wait_ge(s_y2out, b * 16 + 32)
            v.wait_ge(s_y2T, b + 2)
            hold(v)
            v.tensor_scalar(yS[:, :], lin[:, :], 0.0, dinv[:, bass.ds(b, 1)], ALU.max, ALU.mult).then_inc(s_y2, 1)
            then.end()

        def block1(b, ahead=True):
            then = Chain(s_bch[1], b)

            def share(e):
                v.wait_ge(s_y, b * NEXP + e + 3)
                v.wait_ge(s_yadd, b * NEXP + e + 2)
                if e == NEXP - 1:
                    v.wait_ge(s_out, b * 16 + 32)
                if e == 5:
                    v.wait_ge(s_b2add, b + 2)
                hold(v)
                v.scalar_tensor_tensor((mix if e < NEXP - 1 else res)[:, :], psY[e % 2][:, 0:D], comb[:, e:e + 1],
                                       (mix if e else front)[:, :],
                                       ALU.mult, ALU.add).then_inc(s_yadd, 1)

            def biases():
                v.wait_ge(s_b2, b + 2)
                v.wait_ge(s_yadd, b * NEXP + 7)
                hold(v)
                v.tensor_tensor(mix[:, :], psG[:, 0:D], mix[:, :], ALU.add).then_inc(s_b2add, 1)

            def newton():
                then(v.tensor_scalar(nt1[:, :], rs[:, :], rs[:, :], var1[:, :], ALU.mult, ALU.mult))
                then(v.tensor_scalar(nt2[:, :], nt1[:, :], -0.5, 1.5, ALU.mult, ALU.add))
                then(v.tensor_tensor(rs[:, :], rs[:, :], nt2[:, :], ALU.mult))

            def weights():
                then(v.tensor_copy(topf[:, :], topi[:, 0:2]))
                v.wait_ge(s_th, b + 1)
                v.wait_ge(s_yadd, b * NEXP + 2)
                hold(v)
                v.tensor_scalar(wts[:, 0:1], th[:, :], 0.5, 0.5, ALU.mult, ALU.add)
                then(v.tensor_scalar(wts[:, 1:2], th[:, :], -0.5, 0.5, ALU.mult, ALU.add))
                v.tensor_scalar(pick[:, :], iota[:, 0:NEXP], topf[:, 0:1], wts[:, 0:1], ALU.is_equal, ALU.mult)
                then(v.tensor_scalar(comb[:, :], iota[:, 0:NEXP], topf[:, 1:2], wts[:, 1:2], ALU.is_equal, ALU.mult))
                v.tensor_tensor(comb[:, :], comb[:, :], pick[:, :], ALU.add).then_inc(s_comb, 1)
                v.wait_ge(s_comb, b + 1)
                hold(v)

            weights()
            if not ahead:
                for e in range(5):
                    share(e)
                biases()
                for e in range(5, NEXP):
                    share(e)
                return
            linear(1, b, then)
            v.sem_inc(s_linread, 1)
            v.wait_ge(s_x, b * 16 + 16)
            hold(v)
            then(v.scalar_tensor_tensor(x2[:, :], lin[:, :], 0.0, xS[:, :], ALU.max, ALU.add))
            share(0)
            then(v.bn_stats(st1[:, :], x2[:, :]))
            then(v.bn_aggr(mv1[:, :], st1[:, :]))
            then(v.tensor_scalar(var1[:, :], mv1[:, 1:2], EPS, None, ALU.add))
            then(v.tensor_scalar(halfi[:, :], var1[:, :].bitcast(I32), 1, None, ALU.arith_shift_right))
            share(1)
            then(v.tensor_scalar(rs[:, :].bitcast(I32), halfi[:, :], -1.0, float(0x5f3759df), ALU.mult, ALU.add))
            newton()
            share(2)
            newton()
            share(3)
            newton()
            v.tensor_scalar(tok[:, :], x2[:, :], mv1[:, 0:1], rs[:, :], ALU.subtract, ALU.mult).then_inc(s_tok, 1)
            share(4)
            biases()
            v.wait_ge(s_tok, b + 2)
            hold(v)
            then(v.tensor_tensor(front[:, :], x2[:, :], tok[:, :], ALU.add))
            share(5)
            share(6)
            v.wait_ge(s_lg, b + 1)
            hold(v)
            then(v.tensor_copy(lg[:, :], psT[:, 256:256 + NEXP]))
            then(v.max(top[:, :], lg[:, :]))
            v.tensor_tensor(gap[:, :], top[:, 0:1], top[:, 1:2], ALU.subtract).then_inc(s_gap, 1)
            then(v.max_index(topi[:, :], top[:, :], lg[:, :]))
            share(7)
            then.end()

        v.wait_ge(s_y2out, 16)
        v.wait_ge(s_out, 16)
        for l in range(2):
            if l == 0:
                v.wait_ge(s_y1C, NB + XS)
            else:
                v.wait_ge(s_y2C, NB + 2)
            body = (block0, block1)[l]
            if l == 0:
                for r in range(R):
                    selection(0, r)
            with v.Fori(0, NI) as i:
                words = record(v, i, REC_X, REC - REC_X, NG * (NP // W), counted=False)
                xs = words[0:R + 1]
                bases = [w.with_bounds(min_val=0, max_val=NP - LO) for w in words[REC_B - REC_X:REC_B - REC_X + R]]
                ahead = v.snap((i + 1) % NI)
                g0 = (i + l * NI) * R
                with v.If(xs[R] > xs[0]):
                    xs = record(v, i, REC_X, R + 1, NG * (NP // W))
                    for r in range(R):
                        add(g0 + r, r, bases[r])
                    v.wait_ge(s_added, g0 + (R + 2))
                    hold(v)
                    for r in range(R):
                        with v.If(xs[r + 1] > xs[r]):
                            further(l, i, r, xs, bases[r])
                        hold(v)
                    v.sem_inc(s_free, R)
                    for r in range(R):
                        selection(ahead, r)
                with v.Else():
                    for r in range(R):
                        add(g0 + r, r, bases[r])
                        v.sem_inc(s_free, 1)
                        selection(ahead, r)
                    v.wait_ge(s_added, g0 + (R + 2))
                    hold(v)
                v.sem_inc(s_iter, 1)
                e0, e1 = record(v, i, REC_E, 2, NB)
                with v.If(e1 > e0):
                    with v.Fori(e0, e1) as b:
                        body(b.with_bounds(min_val=0, max_val=NB - 1))
            with v.Fori(record(v, NI - 1, REC_E + 1, 1, NB - 1)[0], NB) as b:
                body(b.with_bounds(min_val=0, max_val=NB - 1))
        block1(NB, ahead=False)

    ctx.close()


_INS = ["x", "src", "dst", "edge_weight", "L0_gnn_W1", "L0_gnn_b1", "L0_gnn_W2", "L0_gnn_b2",
        "L0_ffn_router_w", "L0_ffn_w1", "L0_ffn_b1", "L0_ffn_w2", "L0_ffn_b2"]


def kernel(**inputs):
    import numpy as np
    import concourse.bacc as bacc
    from concourse.bass_utils import run_bass_kernel_spmd

    nc = bacc.Bacc("TRN2", target_bir_lowering=False, num_devices=1)
    arrays, args = {}, []
    for name in _INS:
        a = np.ascontiguousarray(inputs[name])
        arrays[f"in_{name}"] = a
        args.append(nc.dram_tensor(f"in_{name}", a.shape, mybir.dt.from_np(a.dtype), kind="ExternalInput").ap())
    out = nc.dram_tensor("out", [N, D], F32, kind="ExternalOutput").ap()
    build(nc, *args, out)
    r = run_bass_kernel_spmd(nc, [arrays], core_ids=[0])
    return r.results[0]["out"]
```
